# Optimizing a Trainium2 kernel written in Bass

```python
import numpy as np
import jax
import jax.numpy as jnp

def _softmax(x, axis=-1):
    return jax.nn.softmax(x, axis=axis)

def _gelu(x):
    return jax.nn.gelu(x, approximate=True)

def _silu(x):
    return jax.nn.silu(x)

def _sigmoid(x):
    return jax.nn.sigmoid(x)

def _layernorm(x, axis=-1, eps=1e-05):
    m = jnp.mean(x, axis=axis, keepdims=True)
    v = jnp.var(x, axis=axis, keepdims=True)
    return (x - m) / jnp.sqrt(v + eps)

def _scatter_add(tgt, idx, src, axis=0):
    return tgt.at[idx].add(src)

def _segment_sum(src, seg, n):
    return jax.ops.segment_sum(src, seg, n)
kernel_name = 'mk_prb_d1_jaxref_r8_4b669b'

def setup_inputs(seed: int=0):
    np.random.seed(seed)
    _w = jnp.asarray

    def _L0_attn_setup():
        import jax, jax.numpy as jnp
        import numpy as np
        HIDDEN = 128
        NUM_HEADS = 16
        HEAD_SIZE = 64
        key = jax.random.key(seed)
        ks = jax.random.split(key, 5)
        B, S = (2, 256)
        scale = 1.0 / np.sqrt(HIDDEN)
        x = jax.random.normal(ks[0], (B, S, HIDDEN), dtype=jnp.float32)
        W_qkv = jax.random.normal(ks[1], (HIDDEN, 3 * NUM_HEADS * HEAD_SIZE), dtype=jnp.float32) * scale
        b_qkv = jnp.zeros((3 * NUM_HEADS * HEAD_SIZE,), dtype=jnp.float32)
        W_out = jax.random.normal(ks[2], (NUM_HEADS * HEAD_SIZE, HIDDEN), dtype=jnp.float32) * scale
        b_out = jnp.zeros((HIDDEN,), dtype=jnp.float32)
        return {'x': x, 'W_qkv': W_qkv, 'b_qkv': b_qkv, 'W_out': W_out, 'b_out': b_out}
    _L0_attn_in = _L0_attn_setup()

    def _L0_ffn_setup():
        import jax, jax.numpy as jnp
        import numpy as np
        DIM = 128
        DEPTH = 2
        HEADS = 8
        DIM_HEAD = 64
        WINDOW = 64
        INNER = HEADS * DIM_HEAD
        HID = int(DIM * 4 * 2 / 3)
        B, N = (2, 1024)
        QK_SCALE = 8.0

        def shift_token(t):
            t1, t2 = jnp.split(t, 2, axis=-1)
            t2 = jnp.pad(t2, ((0, 0), (1, 0), (0, 0)))[:, :-1]
            return jnp.concatenate([t1, t2], axis=-1)

        def l2norm(t):
            return t / jnp.clip(jnp.linalg.norm(t, axis=-1, keepdims=True), 1e-12)

        def rotate_half(x):
            x1, x2 = jnp.split(x, 2, axis=-1)
            return jnp.concatenate([-x2, x1], axis=-1)

        def rotary_xpos(q, k):
            n = q.shape[-2]
            half_idx = jnp.arange(0, DIM_HEAD, 2, dtype=jnp.float32)
            inv_freq = 1.0 / 10000.0 ** (half_idx / DIM_HEAD)
            t = jnp.arange(n, dtype=jnp.float32)
            freqs = t[:, None] * inv_freq[None, :]
            freqs = jnp.concatenate([freqs, freqs], axis=-1)
            base = (half_idx + 0.4 * DIM_HEAD) / (1.4 * DIM_HEAD)
            power = (t - n // 2) / float(WINDOW // 2)
            scale = base[None, :] ** power[:, None]
            scale = jnp.concatenate([scale, scale], axis=-1)
            cos, sin = (jnp.cos(freqs), jnp.sin(freqs))
            q = q * cos * scale + rotate_half(q) * sin * scale
            k = k * cos / scale + rotate_half(k) * sin / scale
            return (q, k)

        def local_attention(q, k, v):
            b, h, n, d = q.shape
            w = n // WINDOW
            bq = q.reshape(b, h, w, WINDOW, d) * QK_SCALE
            bk = k.reshape(b, h, w, WINDOW, d)
            bv = v.reshape(b, h, w, WINDOW, d)

            def look_around(t):
                p = jnp.pad(t, ((0, 0), (0, 0), (1, 0), (0, 0), (0, 0)))
                return jnp.concatenate([p[:, :, :w], p[:, :, 1:]], axis=3)
            bk, bv = (look_around(bk), look_around(bv))
            bt = jnp.arange(n).reshape(w, WINDOW)
            btp = jnp.pad(bt, ((1, 0), (0, 0)), constant_values=-1)
            btk = jnp.concatenate([btp[:w], btp[1:]], axis=1)
            sim = jnp.einsum('bhwid,bhwjd->bhwij', bq, bk)
            i = bt[:, :, None]
            j = btk[:, None, :]
            mask = (i < j) | (i > j + WINDOW) | (j == -1)
            sim = jnp.where(mask, -jnp.finfo(sim.dtype).max, sim)
            attn = jax.nn.softmax(sim, axis=-1)
            out = jnp.einsum('bhwij,bhwjd->bhwid', attn, bv)
            return out.reshape(b, h, n, d)

        def _layer(x, wqkv, qs, ksc, wo, lg, lb, w1, b1, w2, b2):
            b, n, _ = x.shape
            h = shift_token(x)
            qkv = h @ wqkv
            q, k, v = jnp.split(qkv, 3, axis=-1)
            to_heads = lambda t: t.reshape(b, n, HEADS, DIM_HEAD).transpose(0, 2, 1, 3)
            q, k, v = (to_heads(q), to_heads(k), to_heads(v))
            q = l2norm(q) * qs
            k = l2norm(k) * ksc
            q, k = rotary_xpos(q, k)
            o = local_attention(q, k, v)
            o = o.transpose(0, 2, 1, 3).reshape(b, n, INNER)
            x = x + o @ wo
            h = shift_token(x)
            mu = h.mean(-1, keepdims=True)
            var = h.var(-1, keepdims=True)
            h = (h - mu) / jnp.sqrt(var + 1e-05) * lg + lb
            h = h @ w1 + b1
            a, g = jnp.split(h, 2, axis=-1)
            h = a * jax.nn.gelu(g, approximate=False)
            x = x + h @ w2 + b2
            return x
        key = jax.random.key(seed)
        ks = jax.random.split(key, 6)
        return {'x': jax.random.normal(ks[0], (B, N, DIM), jnp.float32), 'wqkv': jax.random.normal(ks[1], (DEPTH, DIM, 3 * INNER), jnp.float32) * 0.02, 'q_scale': jnp.ones((DEPTH, DIM_HEAD), jnp.float32), 'k_scale': jnp.ones((DEPTH, DIM_HEAD), jnp.float32), 'wo': jax.random.normal(ks[2], (DEPTH, INNER, DIM), jnp.float32) * 0.02, 'ln_g': jnp.ones((DEPTH, DIM), jnp.float32), 'ln_b': jnp.zeros((DEPTH, DIM), jnp.float32), 'w1': jax.random.normal(ks[3], (DEPTH, DIM, 2 * HID), jnp.float32) * 0.02, 'b1': jnp.zeros((DEPTH, 2 * HID), jnp.float32), 'w2': jax.random.normal(ks[4], (DEPTH, HID, DIM), jnp.float32) * 0.02, 'b2': jnp.zeros((DEPTH, DIM), jnp.float32)}
    _L0_ffn_in = _L0_ffn_setup()
    _d = {'L0_attn_x': _L0_attn_in['x'], 'L0_attn_W_qkv': _L0_attn_in['W_qkv'], 'L0_attn_b_qkv': _L0_attn_in['b_qkv'], 'L0_attn_W_out': _L0_attn_in['W_out'], 'L0_attn_b_out': _L0_attn_in['b_out'], 'L0_ffn_wqkv': _L0_ffn_in['wqkv'], 'L0_ffn_q_scale': _L0_ffn_in['q_scale'], 'L0_ffn_k_scale': _L0_ffn_in['k_scale'], 'L0_ffn_wo': _L0_ffn_in['wo'], 'L0_ffn_ln_g': _L0_ffn_in['ln_g'], 'L0_ffn_ln_b': _L0_ffn_in['ln_b'], 'L0_ffn_w1': _L0_ffn_in['w1'], 'L0_ffn_b1': _L0_ffn_in['b1'], 'L0_ffn_w2': _L0_ffn_in['w2'], 'L0_ffn_b2': _L0_ffn_in['b2']}
    _x0 = _d['L0_attn_x']
    _d['L0_attn_x'] = jax.random.normal(jax.random.fold_in(jax.random.key(seed), 1), (16, 512, 128), dtype=_x0.dtype)
    del _x0
    return _d

def reference(L0_attn_x, L0_attn_W_qkv, L0_attn_b_qkv, L0_attn_W_out, L0_attn_b_out, L0_ffn_wqkv, L0_ffn_q_scale, L0_ffn_k_scale, L0_ffn_wo, L0_ffn_ln_g, L0_ffn_ln_b, L0_ffn_w1, L0_ffn_b1, L0_ffn_w2, L0_ffn_b2):

    def _L0_attn_ref(x, W_qkv, b_qkv, W_out, b_out):
        import jax, jax.numpy as jnp
        import numpy as np
        HIDDEN = 128
        NUM_HEADS = 16
        HEAD_SIZE = 64
        B, S, _ = x.shape
        qkv = x @ W_qkv + b_qkv
        qkv = qkv.reshape(B, S, 3 * NUM_HEADS, HEAD_SIZE)
        Q = qkv[:, :, :NUM_HEADS, :]
        K = qkv[:, :, NUM_HEADS:2 * NUM_HEADS, :]
        V = qkv[:, :, 2 * NUM_HEADS:, :]
        scores = jnp.einsum('bqhi,bkhi->bhqk', Q, K) / jnp.sqrt(jnp.float32(HEAD_SIZE))
        mask = jnp.triu(jnp.full((S, S), -10000.0, dtype=scores.dtype), k=1)
        scores = scores + mask
        probs = jax.nn.softmax(scores, axis=-1)
        vals = jnp.einsum('bkhi,bhqk->bqhi', V, probs)
        vals = vals.reshape(B, S, NUM_HEADS * HEAD_SIZE)
        return vals @ W_out + b_out

    def _L0_ffn_ref(x, wqkv, q_scale, k_scale, wo, ln_g, ln_b, w1, b1, w2, b2):
        import jax, jax.numpy as jnp
        import numpy as np
        DIM = 128
        DEPTH = 2
        HEADS = 8
        DIM_HEAD = 64
        WINDOW = 64
        INNER = HEADS * DIM_HEAD
        HID = int(DIM * 4 * 2 / 3)
        B, N = (2, 1024)
        QK_SCALE = 8.0

        def shift_token(t):
            t1, t2 = jnp.split(t, 2, axis=-1)
            t2 = jnp.pad(t2, ((0, 0), (1, 0), (0, 0)))[:, :-1]
            return jnp.concatenate([t1, t2], axis=-1)

        def l2norm(t):
            return t / jnp.clip(jnp.linalg.norm(t, axis=-1, keepdims=True), 1e-12)

        def rotate_half(x):
            x1, x2 = jnp.split(x, 2, axis=-1)
            return jnp.concatenate([-x2, x1], axis=-1)

        def rotary_xpos(q, k):
            n = q.shape[-2]
            half_idx = jnp.arange(0, DIM_HEAD, 2, dtype=jnp.float32)
            inv_freq = 1.0 / 10000.0 ** (half_idx / DIM_HEAD)
            t = jnp.arange(n, dtype=jnp.float32)
            freqs = t[:, None] * inv_freq[None, :]
            freqs = jnp.concatenate([freqs, freqs], axis=-1)
            base = (half_idx + 0.4 * DIM_HEAD) / (1.4 * DIM_HEAD)
            power = (t - n // 2) / float(WINDOW // 2)
            scale = base[None, :] ** power[:, None]
            scale = jnp.concatenate([scale, scale], axis=-1)
            cos, sin = (jnp.cos(freqs), jnp.sin(freqs))
            q = q * cos * scale + rotate_half(q) * sin * scale
            k = k * cos / scale + rotate_half(k) * sin / scale
            return (q, k)

        def local_attention(q, k, v):
            b, h, n, d = q.shape
            w = n // WINDOW
            bq = q.reshape(b, h, w, WINDOW, d) * QK_SCALE
            bk = k.reshape(b, h, w, WINDOW, d)
            bv = v.reshape(b, h, w, WINDOW, d)

            def look_around(t):
                p = jnp.pad(t, ((0, 0), (0, 0), (1, 0), (0, 0), (0, 0)))
                return jnp.concatenate([p[:, :, :w], p[:, :, 1:]], axis=3)
            bk, bv = (look_around(bk), look_around(bv))
            bt = jnp.arange(n).reshape(w, WINDOW)
            btp = jnp.pad(bt, ((1, 0), (0, 0)), constant_values=-1)
            btk = jnp.concatenate([btp[:w], btp[1:]], axis=1)
            sim = jnp.einsum('bhwid,bhwjd->bhwij', bq, bk)
            i = bt[:, :, None]
            j = btk[:, None, :]
            mask = (i < j) | (i > j + WINDOW) | (j == -1)
            sim = jnp.where(mask, -jnp.finfo(sim.dtype).max, sim)
            attn = jax.nn.softmax(sim, axis=-1)
            out = jnp.einsum('bhwij,bhwjd->bhwid', attn, bv)
            return out.reshape(b, h, n, d)

        def _layer(x, wqkv, qs, ksc, wo, lg, lb, w1, b1, w2, b2):
            b, n, _ = x.shape
            h = shift_token(x)
            qkv = h @ wqkv
            q, k, v = jnp.split(qkv, 3, axis=-1)
            to_heads = lambda t: t.reshape(b, n, HEADS, DIM_HEAD).transpose(0, 2, 1, 3)
            q, k, v = (to_heads(q), to_heads(k), to_heads(v))
            q = l2norm(q) * qs
            k = l2norm(k) * ksc
            q, k = rotary_xpos(q, k)
            o = local_attention(q, k, v)
            o = o.transpose(0, 2, 1, 3).reshape(b, n, INNER)
            x = x + o @ wo
            h = shift_token(x)
            mu = h.mean(-1, keepdims=True)
            var = h.var(-1, keepdims=True)
            h = (h - mu) / jnp.sqrt(var + 1e-05) * lg + lb
            h = h @ w1 + b1
            a, g = jnp.split(h, 2, axis=-1)
            h = a * jax.nn.gelu(g, approximate=False)
            x = x + h @ w2 + b2
            return x
        for l in range(DEPTH):
            x = _layer(x, wqkv[l], q_scale[l], k_scale[l], wo[l], ln_g[l], ln_b[l], w1[l], b1[l], w2[l], b2[l])
        return x
    x = L0_attn_x
    xn = _layernorm(x, axis=-1)
    x = x + _L0_attn_ref(xn, L0_attn_W_qkv, L0_attn_b_qkv, L0_attn_W_out, L0_attn_b_out) + _L0_ffn_ref(xn, L0_ffn_wqkv, L0_ffn_q_scale, L0_ffn_k_scale, L0_ffn_wo, L0_ffn_ln_g, L0_ffn_ln_b, L0_ffn_w1, L0_ffn_b1, L0_ffn_w2, L0_ffn_b2)
    return x

_drawn_inputs = setup_inputs


def setup_inputs(seed=0):
    import zlib

    import numpy as np

    out = dict(_drawn_inputs(seed))
    spreads = {'L0_attn_b_qkv': (0.0, 0.408),
     'L0_attn_b_out': (0.0, 0.8),
     'L0_ffn_q_scale': (1.0, 0.6),
     'L0_ffn_k_scale': (1.0, 0.6),
     'L0_ffn_ln_g': (1.0, 0.6),
     'L0_ffn_ln_b': (0.0, 0.8),
     'L0_ffn_b1': (0.0, 0.8),
     'L0_ffn_b2': (0.0, 0.477)}
    factors = {'L0_ffn_wqkv': 3.897, 'L0_ffn_wo': 3.897, 'L0_ffn_w1': 6.45, 'L0_ffn_w2': 6.357}
    for name, (base, spread) in spreads.items():
        noise = np.random.default_rng([zlib.crc32(name.encode()), seed]).standard_normal(out[name].shape)
        drawn = base * np.exp(spread * noise) if base else spread * noise
        out[name] = jnp.asarray(drawn.astype(out[name].dtype))
    for name, factor in factors.items():
        out[name] = (out[name] * factor).astype(out[name].dtype)
    return out
```

```python
import numpy as np
from contextlib import ExitStack

import concourse.bass as bass
from concourse import mybir

F32 = mybir.dt.float32
F32R = mybir.dt.float32r
BF16 = mybir.dt.bfloat16
ALU = mybir.AluOpType
ACT = mybir.ActivationFunctionType
AX = mybir.AxisListType

BATCH, SEQ, DIM = 16, 512, 128
P = 128
TILES = SEQ // P
HEAD = 64
HEADS = 16
PAIRS = HEADS * HEAD // P
WINDOW = 64
DEPTH = 2
LHEADS = 8
LPAIRS = LHEADS * HEAD // P
INNER = LHEADS * HEAD
HID = int(DIM * 4 * 2 / 3)
HID_CHUNKS = [(c, min(P, HID - c)) for c in range(0, HID, P)]
BAND = P + WINDOW
QK_SCALE = 8.0
EPS = 1e-5
MASK_ROW = 16000.0
MASK_CAUSAL = -5.0
MASK_BAND = -float(2.0 ** 110)
CAUSAL_AT = [0, 512, 1024, 896]
CAUSAL_USES = [(0, 512, [(0, 0)]), (512, 512, [(1, 0), (3, 384)]), (1024, 256, [(2, 0)])]
MAX_USES = [[(0, 0), (1, P)], [(2, 0)], [(3, 0)]]


def attention_tasks():
    out = [[("a_proj", 0)], [("a_max", 0)], [("a_neg", 0)]]
    for p in range(PAIRS):
        more = p + 1 < PAIRS
        out += [[("a_proj", p + 1)]] if more else []
        out += [[("a_st", p, 0)]]
        out += [[("a_max", p + 1)]] if more else []
        out += [[("a_st", p, 1)], [("a_pv", p, 0)]]
        out += [[("a_neg", p + 1)]] if more else []
        out += [[("a_pv", p, 1)], [("a_ot", p)], [("a_out", p)]]
    return [t for step in out for t in step]


def local_tasks(l):
    out = [("f_ht", l)]
    out += [("f_qk", l, 0), ("f_v", l, 0)]
    for t in range(1, TILES):
        out += [("f_qk", l, t), ("f_v", l, t), ("f_qkt", l, t - 1)]
    out += [("f_qkt", l, TILES - 1)]
    out += [("f_max", l, 0), ("f_neg", l, 0)]
    for p in range(LPAIRS):
        if p + 1 < LPAIRS:
            out += [("f_max", l, p + 1)]
        out += [("f_st", l, p, 0), ("f_st", l, p, 1), ("f_pv", l, p, 0)]
        if p + 1 < LPAIRS:
            out += [("f_neg", l, p + 1)]
        out += [("f_pv", l, p, 1), ("f_ot", l, p)]
    out += [("f_wo", l), ("f_ln", l)]
    out += [("f_up", l, j) for j in range(len(HID_CHUNKS))]
    out += [("f_down", l)]
    return out


def merged(a, b):
    out, n, m = [], 0, 0
    while n < len(a) or m < len(b):
        if m >= len(b) or (n < len(a) and n * len(b) <= m * len(a)):
            out.append(a[n])
            n += 1
        else:
            out.append(b[m])
            m += 1
    return out


SCHEDULE = [("in",)] + merged(attention_tasks(), local_tasks(0) + local_tasks(1)) + [("out",)]


def earlier(task, which):
    at = SCHEDULE.index(task)
    for k in range(at - 1, at - 1 - len(SCHEDULE), -1):
        if which(SCHEDULE[k]):
            return SCHEDULE[k], k < 0
    raise ValueError(task)


class Signal:

    def __init__(self, sem, marks):
        self.sem = sem
        self.names = [(task, m) for task in SCHEDULE for m in marks.get(task[0], ())]
        self.at = {n: k + 1 for k, n in enumerate(self.names)}
        self.count = len(self.names)

    def now(self, i, task, mark):
        return i * self.count + (self.count + self.at[task, mark])

    def before(self, i, task, mark):
        return i * self.count + self.at[task, mark]


class Ring:

    def __init__(self, banks, filled, read, marks):
        self.banks, self.filled, self.read = banks, filled, read
        n = len(banks)
        self.use = {}
        self.per_slot = [0] * n
        k = 0
        for task in SCHEDULE:
            for m in marks.get(task[0], ()):
                self.per_slot[k % n] += 1
                self.use[task, m] = (k % n, self.per_slot[k % n])
                k += 1

    def bank(self, task, mark):
        return self.banks[self.use[task, mark][0]]

    def wait_filled(self, engine, i, task, mark, before=False):
        slot, k = self.use[task, mark]
        per = self.per_slot[slot]
        engine.wait_ge(self.filled[slot], i * per + (k if before else per + k))

    def wait_read(self, engine, i, task, mark, before=False):
        slot, k = self.use[task, mark]
        per = self.per_slot[slot]
        engine.wait_ge(self.read[slot], i * per + (k if before else per + k))

    def wait_all_read(self, engine, i, uses):
        last = {self.use[u][0]: u for u in sorted(uses, key=lambda u: self.use[u][1])}
        for task, mark in last.values():
            self.wait_read(engine, i, task, mark)

    def claim(self, engine, i, task, mark):
        slot, k = self.use[task, mark]
        engine.wait_ge(self.read[slot], i * self.per_slot[slot] + (self.per_slot[slot] + k - 1))
        return self.banks[slot]

    def raise_filled(self, ins, task, mark):
        ins.then_inc(self.filled[self.use[task, mark][0]], 1)

    def raise_read(self, ins, task, mark):
        ins.then_inc(self.read[self.use[task, mark][0]], 1)


def rope_tables():
    half = np.arange(0, HEAD, 2, dtype=np.float32)
    inv_freq = (np.float32(1.0) / np.float32(10000.0) ** (half / np.float32(HEAD))).astype(np.float32)
    t = np.arange(SEQ, dtype=np.float32)
    freqs = t[:, None] * inv_freq[None, :]
    freqs = np.concatenate([freqs, freqs], axis=-1)
    base = (half + np.float32(0.4 * HEAD)) / np.float32(1.4 * HEAD)
    power = (t - np.float32(SEQ // 2)) / np.float32(WINDOW // 2)
    scale = base[None, :] ** power[:, None]
    scale = np.concatenate([scale, scale], axis=-1)
    cos, sin = np.cos(freqs), np.sin(freqs)
    sign = np.concatenate([-np.ones(HEAD // 2), np.ones(HEAD // 2)]).astype(np.float32)[None, :]
    out = np.stack([cos * scale * np.float32(QK_SCALE), sin * sign * scale * np.float32(QK_SCALE),
                    cos / scale, sin * sign / scale])
    return out.astype(np.float32)


def prenorm_attention_and_local_transformer(nc, x, W_qkv, b_qkv, W_out, b_out, wqkv, q_scale, k_scale,
                                            wo, ln_g, ln_b, w1, b1, w2, b2, rope, out):
    ctx = ExitStack()
    with ctx:
        def sb(name, shape, dt=F32):
            return ctx.enter_context(nc.sbuf_tensor(name, shape, dt))

        def sem(name):
            return ctx.enter_context(nc.semaphore(name))

        Wqkv = [sb(f"Wqkv_{s}", [P, 3 * HEADS * HEAD], F32R) for s in ("hi", "lo")]
        Wout = [sb(f"Wout_{s}", [P, PAIRS, DIM], F32R) for s in ("hi", "lo")]
        Lqkv = [[sb(f"Lqkv{l}_{s}", [P, 3 * INNER], F32R) for s in ("hi", "lo")] for l in range(DEPTH)]
        Lwo = [[sb(f"Lwo{l}_{s}", [P, LPAIRS, DIM], F32R) for s in ("hi", "lo")] for l in range(DEPTH)]
        Lw1 = [[sb(f"Lw1{l}_{s}", [P, 2 * HID], F32R) for s in ("hi", "lo")] for l in range(DEPTH)]
        Lw2 = [[sb(f"Lw2{l}_{s}", [P, len(HID_CHUNKS), DIM], F32R) for s in ("hi", "lo")] for l in range(DEPTH)]
        bqkv = sb("bqkv", [P, 3 * PAIRS])
        bout = sb("bout", [P, 1])
        lng, lnb = sb("lng", [P, DEPTH]), sb("lnb", [P, DEPTH])
        b1s = sb("b1s", [P, DEPTH, 2, len(HID_CHUNKS)])
        b2s = sb("b2s", [P, DEPTH, DIM])
        rope_t = sb("rope_t", [P, DEPTH, 4, TILES, HEAD])

        ident = sb("ident", [P, P])
        identb = sb("identb", [P, P], BF16)
        mask_row = sb("mask_row", [P, P], BF16)
        future_q = sb("future_q", [P, P], BF16)
        future_k = sb("future_k", [P, P], BF16)
        band = sb("band", [P, 3, BAND], BF16)
        pick = sb("pick", [2, 2, P], BF16)
        minus_half = sb("minus_half", [P, LHEADS])
        zero_row = sb("zero_row", [1, DIM // 2])

        x_in = sb("x_in", [P, TILES, DIM])
        x_res = sb("x_res", [P, TILES, DIM])
        xl = sb("xl", [P, TILES, DIM])
        xT = [sb(f"xT_{s}", [P, SEQ], F32R) for s in ("hi", "lo")]
        h = sb("h", [P, TILES, DIM])
        hT = [sb(f"hT_{s}", [P, SEQ], F32R) for s in ("hi", "lo")]
        stats = sb("stats", [P, TILES, 6])
        mv = sb("mv", [P, TILES, 2])
        var_eps = sb("var_eps", [P, TILES])
        rstd = sb("rstd", [P, TILES])
        Qa = [[sb(f"Qa{b}_{s}", [P, SEQ], F32R) for s in ("hi", "lo")] for b in range(2)]
        Ka = [[sb(f"Ka{b}_{s}", [P, SEQ], F32R) for s in ("hi", "lo")] for b in range(2)]
        Va = [sb(f"Va{b}", [P, TILES, 2, HEAD + 1]) for b in range(2)]
        neg = [sb(f"neg{b}", [P, TILES, 2], BF16) for b in range(2)]
        negT = [sb(f"negT{b}", [2, SEQ], BF16) for b in range(2)]
        probs = [sb(f"probs{b}", [P, 1280]) for b in range(2)]
        Oa = sb("Oa", [P, TILES, P])
        OaT = [sb(f"OaT_{s}", [P, SEQ], F32R) for s in ("hi", "lo")]
        rec_a = sb("rec_a", [P, TILES])
        aT = Oa[:, :, :].rearrange("p t n -> p (t n)")
        Qf = [sb(f"Qf_{s}", [P, LPAIRS, SEQ], F32R) for s in ("hi", "lo")]
        Kf = [sb(f"Kf_{s}", [P, LPAIRS, SEQ], F32R) for s in ("hi", "lo")]
        Vf = sb("Vf", [P, TILES, LHEADS, HEAD + 1])
        negf = [sb(f"negf{b}", [P, TILES, 2], BF16) for b in range(2)]
        negfT = [sb(f"negfT{b}", [2, SEQ], BF16) for b in range(2)]
        lprobs = [sb(f"lprobs{b}", [P, 4 * BAND - WINDOW]) for b in range(2)]
        scales = lprobs[0][:, 0:DEPTH * 4 * HEAD].rearrange("p (l k d) -> p l k d", l=DEPTH, k=4)
        Of = sb("Of", [P, TILES, P])
        rec_f = sb("rec_f", [P, TILES])
        scratch = sb("scratch", [P, 4, SEQ])
        qkn = [Of[:, :, :].rearrange("p t n -> p (t n)"), sb("kn", [P, INNER])[:, :]]
        ss = sb("ss", [P, LHEADS])
        ssc = [sb(f"ssc{s}", [P, LHEADS]) for s in range(2)]
        rnorm = [sb(f"rnorm{s}", [P, LHEADS]) for s in range(2)]
        squares, turn_a, turn_b, turned = (scratch[:, k] for k in range(4))
        ln_tmp, gate, glu = scratch[:, 3], scratch[:, 0], scratch[:, 1]
        out_a = scratch[:, 2].rearrange("p (t d) -> p t d", t=TILES)
        OfT, GLU = Qf, Kf

        banks = [ctx.enter_context(nc.psum_tensor(f"bank{k}", [P, 512], F32)) for k in range(8)]

        def ring(name, at, n, marks):
            return Ring(banks[at:at + n], [sem(f"{name}_filled{k}") for k in range(n)],
                        [sem(f"{name}_read{k}") for k in range(n)], marks)

        work = ring("work", 0, 2, dict(
            a_proj="qkv", a_neg="m", a_ot="o", f_ht="h", f_qk="qk", f_v="v", f_qkt="qk", f_neg="m", f_ot="o",
            f_wo="w", f_ln="h", f_up="ga", f_down="d", out="t", **{"in": "x"}))
        maxima = ring("maxima", 2, 2, dict(a_max=[(j, u) for j in range(2) for u in range(3)],
                                           f_max=[(j, u) for j in range(2) for u in range(2)]))
        score = ring("score", 4, 2, dict(a_st=[0, 1, 2], f_st=[0, 1]))
        value = ring("value", 6, 1, dict(a_pv="v", f_pv="v"))
        out_acc = banks[7]

        hi_ready = Signal(sem("hi_ready"), dict(
            a_proj="qk", a_ot="o", f_ht="h", f_qkt="qk", f_ot="o", f_ln="h", f_up="g", **{"in": "x"}))
        lo_ready = Signal(sem("lo_ready"), dict(f_ln="h", f_up="g"))
        squares_ready = Signal(sem("squares_ready"), dict(f_qk="qk"))
        rec_ready = Signal(sem("rec_ready"), dict(a_pv="r", f_pv="r"))
        turn_ready = Signal(sem("turn_ready"), dict(f_qk="qk"))
        clip_ready = Signal(sem("clip_ready"), dict(f_qk="qk"))
        norm_ready = Signal(sem("norm_ready"), dict(f_ln="saen", **{"in": "saen"}))
        rstd_ready = Signal(sem("rstd_ready"), dict(f_ln="p", **{"in": "p"}))
        rnorm_ready = Signal(sem("rnorm_ready"), dict(f_qk="qk"))
        turned_ready = Signal(sem("turned_ready"), dict(f_qk="qk"))
        qk_ready = Signal(sem("qk_ready"), dict(f_qk="qk"))
        copy_ready = Signal(sem("copy_ready"), dict(**{"in": "cx"}))
        bias_ready = Signal(sem("bias_ready"), dict(f_ln="b"))
        sum_ready = Signal(sem("sum_ready"), dict(out="o"))
        out_ready = Signal(sem("out_ready"), dict(a_out="a"))
        aT_ready = Signal(sem("aT_ready"), dict(out="a"))
        own = {
            "act": [hi_ready, squares_ready],
            "dve": [lo_ready, rec_ready, turn_ready, clip_ready, norm_ready, aT_ready],
            "pool": [rstd_ready, rnorm_ready, turned_ready, qk_ready, copy_ready, bias_ready, sum_ready],
            "pe": [out_ready]}
        x_loaded, shifted, stored, zeroed = sem("x_loaded"), sem("shifted"), sem("stored"), sem("zeroed")
        staged = [sem(f"staged{k}") for k in range(4)]
        split_hi, split_lo = sem("split_hi"), sem("split_lo")
        carried = {engine: sem(f"carried_{engine}") for engine in ("sp", "pool", "dve")}
        params, consts, tables = sem("params"), sem("consts"), sem("tables")

        pieces = []
        for c in range(0, 3 * HEADS * HEAD, 512):
            pieces.append((W_qkv[:, c:c + 512], P, 512, [w[:, c:c + 512] for w in Wqkv]))
        for c in range(0, PAIRS, 4):
            pieces.append((W_out[c * P:(c + 4) * P, :].rearrange("(c p) n -> p c n", p=P), P, 512,
                           [w[:, c:c + 4, :].rearrange("p c n -> p (c n)") for w in Wout]))
        for l in range(DEPTH):
            for c in range(0, 3 * INNER, 512):
                pieces.append((wqkv[l, :, c:c + 512], P, 512, [w[:, c:c + 512] for w in Lqkv[l]]))
            pieces.append((wo[l].rearrange("(c p) n -> p c n", p=P), P, 512,
                           [w[:, :, :].rearrange("p c n -> p (c n)") for w in Lwo[l]]))
            for c in range(0, 2 * HID, 512):
                n = min(512, 2 * HID - c)
                pieces.append((w1[l, :, c:c + n], P, n, [w[:, c:c + n] for w in Lw1[l]]))
            for j, (c, n) in enumerate(HID_CHUNKS):
                pieces.append((w2[l, c:c + n, :], n, DIM, [w[0:n, j, :] for w in Lw2[l]]))

        def stage(k):
            src, rows, n, _ = pieces[k]
            to = scratch[0:rows, k % 4, 0:n]
            return to.rearrange("p (c n) -> p c n", c=src.shape[1]) if len(src.shape) == 3 else to

        def shifts_done(i, task):
            return i * (3 * 16 * 2 * DEPTH) + 3 * 16 * (2 * task[1] + (2 if task[0] == "f_ln" else 1))

        LAST_UP = len(HID_CHUNKS) - 1
        heads = lambda ap: ap.rearrange("p (h d) -> p h d", d=HEAD)
        tiles_of = lambda ap: ap.rearrange("p (t n) -> p t n", t=TILES)

        block = ctx.enter_context(nc.Block())

        @block.sync
        def _(sp):
            count = 0

            def param(dst, src):
                nonlocal count
                sp.dma_start(dst, src, allow_slow_non_contiguous=True).then_inc(params, 16)
                count += 16

            param(bqkv[:, :], b_qkv.rearrange("(c p) -> p c", p=P))
            param(bout[:, :], b_out.rearrange("(p a) -> p a", a=1))
            param(lng[:, :], ln_g.rearrange("l p -> p l"))
            param(lnb[:, :], ln_b.rearrange("l p -> p l"))
            for l in range(DEPTH):
                for half in range(2):
                    for j, (c, m) in enumerate(HID_CHUNKS):
                        at = half * HID + c
                        param(b1s[0:m, l, half, j:j + 1], b1[l, at:at + m].rearrange("(p a) -> p a", a=1))
                param(b2s[:, l, :], b2[l:l + 1, :].broadcast_to([P, DIM]))
                hh = HEAD // 2
                for s, src in enumerate((q_scale, k_scale)):
                    param(scales[:, l, 2 * s, :], src[l:l + 1, :].broadcast_to([P, HEAD]))
                    param(scales[:, l, 2 * s + 1, 0:hh], src[l:l + 1, hh:HEAD].broadcast_to([P, hh]))
                    param(scales[:, l, 2 * s + 1, hh:HEAD], src[l:l + 1, 0:hh].broadcast_to([P, hh]))
                for kind in range(4):
                    param(rope_t[:, l, kind, :, :], rope[kind].rearrange("(t p) d -> p t d", p=P))
            assert count == PARAMS, count
            for k, (src, _, _, _) in enumerate(pieces):
                if k >= 4:
                    sp.wait_ge(split_lo, k - 3)
                sp.dma_start(stage(k), src).then_inc(staged[k % 4], 16)
            half = DIM // 2
            sp.sem_inc(stored, 16)
            with sp.Fori(0, BATCH) as i:
                sp.wait_ge(copy_ready.sem, copy_ready.before(i, ("in",), "c"))
                sp.sem_inc(carried["sp"], 1)
                sp.wait_ge(norm_ready.sem, norm_ready.before(i, ("in",), "n"))
                sp.sem_inc(carried["sp"], 1)
                sp.dma_start(x_in[:, :, :], x[bass.ds(i, 1)].rearrange("a (t p) d -> p (a t) d", p=P)).then_inc(x_loaded, 16)
                for task in SCHEDULE:
                    kind = task[0]
                    if kind in ("f_ht", "f_ln"):
                        if kind == "f_ln":
                            work.wait_read(sp, i, ("f_wo", task[1]), "w")
                            sp.sem_inc(carried["sp"], 1)
                        elif task[1] > 0:
                            work.wait_read(sp, i, ("f_down", task[1] - 1), "d")
                            sp.sem_inc(carried["sp"], 1)
                        else:
                            sp.wait_ge(copy_ready.sem, copy_ready.now(i, ("in",), "x"))
                            sp.sem_inc(carried["sp"], 1)
                            work.wait_filled(sp, i, ("in",), "x")
                            sp.sem_inc(carried["sp"], 1)
                        t0, prev = earlier(task, lambda t: t[0] in ("f_ht", "f_ln"))
                        work.wait_filled(sp, i, t0, "h", prev)
                        sp.sem_inc(carried["sp"], 1)
                        sp.dma_start(h[:, :, 0:half], xl[:, :, 0:half]).then_inc(shifted, 16)
                        sp.dma_start(h[1:P, :, half:DIM], xl[0:P - 1, :, half:DIM]).then_inc(shifted, 16)
                        if kind == "f_ht":
                            sp.dma_start(h[0:1, 0, half:DIM], zero_row[:, :]).then_inc(zeroed, 16)
                        sp.dma_start(h[0:1, 1:TILES, half:DIM], xl[P - 1:P, 0:TILES - 1, half:DIM]).then_inc(shifted, 16)
                    if kind == "out":
                        sp.wait_ge(sum_ready.sem, sum_ready.now(i, task, "o"))
                        sp.sem_inc(carried["sp"], 1)
                        sp.dma_start(out[bass.ds(i, 1)].rearrange("a (t p) d -> p (a t) d", p=P), x_res[:, :, :]).then_inc(stored, 16)
            sp.wait_ge(stored, 16 * BATCH + 16)

        @block.gpsimd
        def _(pool):
            g = nc.gpsimd
            made = [0]

            def const(ins):
                made[0] += 1
                ins.then_inc(consts, 1)
                pool.wait_ge(consts, made[0])

            def select(m, compare, fill, base, pattern, by_row):
                const(g.affine_select(out=m, in_=m, compare_op=compare, fill=fill, base=base, pattern=pattern,
                                      channel_multiplier=by_row))

            const(g.memset(ident[:, :], 0.0))
            select(ident[:, :], ALU.not_equal, 1.0, 0, [[-1, P]], 1)
            const(g.tensor_copy(identb[:, :], ident[:, :]))
            const(g.memset(mask_row[:, :], 0.0))
            select(mask_row[:, :], ALU.not_equal, MASK_ROW, 0, [[-1, P]], 1)
            const(g.memset(future_q[:, :], 0.0))
            select(future_q[:, :], ALU.is_ge, MASK_CAUSAL, 0, [[-1, P]], 1)
            const(g.memset(future_k[:, :], 0.0))
            select(future_k[:, :], ALU.is_ge, MASK_CAUSAL, 0, [[1, P]], -1)
            const(g.memset(band[:, :, :], 0.0))
            const(g.memset(band[:, 0, 0:WINDOW], MASK_BAND))
            select(band[:, :, :], ALU.is_ge, MASK_BAND, 0, [[0, 3], [1, BAND]], -1)
            select(band[:, :, :], ALU.is_ge, MASK_BAND, WINDOW, [[0, 3], [-1, BAND]], 1)
            const(g.memset(pick[:, :, :], 0.0))
            select(pick[:, :, :], ALU.not_equal, 1.0, 0, [[-1, 2], [0, P]], 1)
            const(g.memset(minus_half[:, :], -0.5))
            for b in range(2):
                const(g.memset(Va[b][:, :, :, HEAD:HEAD + 1], 1.0))
            const(g.memset(Vf[:, :, :, HEAD:HEAD + 1], 1.0))
            const(g.memset(zero_row[:, :], 0.0))
            assert made[0] == CONSTS, made[0]
            for sig in own["pool"]:
                pool.sem_inc(sig.sem, sig.count)

            with pool.Fori(0, BATCH) as i:
                for task in SCHEDULE:
                    kind = task[0]
                    if kind in ("in", "f_ln"):
                        pool.wait_ge(norm_ready.sem, norm_ready.now(i, task, "e"))
                        g.tensor_tensor(rstd[:, :], var_eps[:, :], minus_half[:, 0:TILES], ALU.pow).then_inc(rstd_ready.sem, 1)
                    if kind == "in":
                        pool.wait_ge(stored, 16 * i + 16)
                        pool.sem_inc(carried["pool"], 1)
                        g.tensor_copy(x_res[:, :, :], x_in[:, :, :]).then_inc(copy_ready.sem, 1)
                        pool.wait_ge(norm_ready.sem, norm_ready.now(i, task, "n"))
                        work.wait_read(pool, i, ("out",), "t", True)
                        pool.sem_inc(carried["pool"], 1)
                        g.tensor_copy(xl[:, :, :], h[:, :, :]).then_inc(copy_ready.sem, 1)
                    elif kind == "f_ln":
                        pool.wait_ge(shifted, shifts_done(i, task))
                        g.tensor_tensor(xl[:, :, :], xl[:, :, :],
                                        b2s[:, task[1]:task[1] + 1, :].broadcast_to([P, TILES, DIM]),
                                        ALU.add).then_inc(bias_ready.sem, 1)
                    elif kind == "f_qk":
                        for s, c in enumerate("qk"):
                            if s == 1:
                                pool.wait_ge(qk_ready.sem, qk_ready.now(i, task, "q"))
                            else:
                                t0, prev = earlier(task, lambda t: t[0] == "f_qk")
                                pool.wait_ge(qk_ready.sem, (qk_ready.before if prev else qk_ready.now)(i, t0, "k"))
                            pool.wait_ge(clip_ready.sem, clip_ready.now(i, task, c))
                            g.tensor_tensor(rnorm[s][:, :], ssc[s][:, :], minus_half[:, :], ALU.pow).then_inc(rnorm_ready.sem, 1)
                            pool.wait_ge(turn_ready.sem, turn_ready.now(i, task, c))
                            g.tensor_tensor(turned, turn_a, turn_b, ALU.add).then_inc(turned_ready.sem, 1)
                            pool.wait_ge(rnorm_ready.sem, rnorm_ready.now(i, task, c))
                            pool.wait_ge(turned_ready.sem, turned_ready.now(i, task, c))
                            if task[2] > 0:
                                work.wait_filled(pool, i, ("f_qkt", task[1], task[2] - 1), c)
                            g.tensor_tensor(heads(qkn[s]), heads(turned),
                                            rnorm[s][:, :].unsqueeze(2).broadcast_to([P, LHEADS, HEAD]),
                                            ALU.mult).then_inc(qk_ready.sem, 1)
                    elif kind == "out":
                        work.wait_read(pool, i, task, "t")
                        g.tensor_tensor(x_res[:, :, :], x_res[:, :, :], out_a, ALU.add).then_inc(sum_ready.sem, 1)

        @block.scalar
        def _(act):
            a = nc.scalar
            for sig in own["act"]:
                act.sem_inc(sig.sem, sig.count)
            act.wait_ge(params, PARAMS)
            for k, (_, rows, n, parts) in enumerate(pieces):
                act.wait_ge(staged[k % 4], 16 * (k // 4 + 1))
                a.activation(parts[0], scratch[0:rows, k % 4, 0:n], ACT.Copy).then_inc(split_hi, 1)
            act.wait_ge(split_lo, len(pieces))

            def high(i, task, mark, dst, src, func=ACT.Copy, **kw):
                work.wait_filled(act, i, task, mark)
                a.activation(dst, src, func, **kw).then_inc(hi_ready.sem, 1)

            with act.Fori(0, BATCH) as i:
                for task in SCHEDULE:
                    kind = task[0]
                    if kind == "in":
                        work.wait_filled(act, i, ("a_proj", PAIRS - 1), "v", True)
                        high(i, task, "x", xT[0][:, :], work.bank(task, "x")[:, :])
                    elif kind == "a_proj":
                        p = task[1]
                        t0, prev = earlier(task, lambda t: t[0] == "a_st" and t[1] % 2 == p % 2 and t[2] == 1)
                        score.wait_filled(act, i, t0, 2, prev)
                        for c, (m, dst) in enumerate((("q", Qa), ("k", Ka))):
                            high(i, task, m, dst[p % 2][0][:, :], work.bank(task, m)[:, :], ACT.Identity,
                                 bias=bqkv[:, c * PAIRS + p:c * PAIRS + p + 1])
                    elif kind in ("a_neg", "f_neg"):
                        p = task[-1]
                        st, dst = ("a_st", negT) if kind == "a_neg" else ("f_st", negfT)
                        t0, prev = earlier(task, lambda t: t[0] == st and t[-2] % 2 == p % 2 and t[-1] == 1)
                        score.wait_filled(act, i, t0, 2 if kind == "a_neg" else 1, prev)
                        work.wait_filled(act, i, task, "m")
                        work.raise_read(a.activation(dst[p % 2][:, :], work.bank(task, "m")[0:2, :].bitcast(BF16)[:, 0:SEQ],
                                                     ACT.Copy), task, "m")
                    elif kind == "a_st":
                        j = task[2]
                        t0, prev = earlier(task, lambda t: t[0] == "a_pv" and t[2] == j)
                        value.wait_filled(act, i, t0, "v", prev)
                        for u, (at, n, _) in enumerate(CAUSAL_USES):
                            score.wait_filled(act, i, task, u)
                            score.raise_read(a.activation(probs[j][:, at:at + n], score.bank(task, u)[:, 0:n], ACT.Exp,
                                                          scale=float(HEAD) ** -0.5), task, u)
                    elif kind == "f_st":
                        j = task[3]
                        t0, prev = earlier(task, lambda t: t[0] == "f_pv" and t[3] == j)
                        value.wait_filled(act, i, t0, "v", prev)
                        for u, n in enumerate((2 * BAND, BAND + P)):
                            score.wait_filled(act, i, task, u)
                            score.raise_read(a.activation(lprobs[j][:, 2 * BAND * u:2 * BAND * u + n],
                                                          score.bank(task, u)[:, 0:n], ACT.Exp), task, u)
                    elif kind == "a_ot":
                        p = task[1]
                        t0, prev = earlier(task, lambda t: t[0] == "a_out")
                        act.wait_ge(out_ready.sem, (out_ready.before if prev else out_ready.now)(i, t0, "a"))
                        high(i, task, "o", OaT[0][:, :], work.bank(task, "o")[:, :], ACT.Identity,
                             bias=bqkv[:, 2 * PAIRS + p:2 * PAIRS + p + 1])
                    elif kind == "f_ht":
                        t0, prev = earlier(task, lambda t: t[0] == "f_up" and t[2] == LAST_UP)
                        work.wait_filled(act, i, t0, "a", prev)
                        high(i, task, "h", hT[0][:, :], work.bank(task, "h")[:, :])
                    elif kind == "f_qk":
                        for s, c in enumerate("qk"):
                            if s == 1:
                                work.wait_read(act, i, task, "q")
                            else:
                                t0, prev = earlier(task, lambda t: t[0] == "f_qk" or t == ("f_up", (task[1] - 1) % DEPTH, LAST_UP))
                                work.wait_read(act, i, t0, "k" if t0[0] == "f_qk" else "a", prev)
                            work.wait_filled(act, i, task, c)
                            a.activation(squares, work.bank(task, c)[:, :], ACT.Square).then_inc(squares_ready.sem, 1)
                    elif kind == "f_v":
                        t0, prev = earlier(task, lambda t: t[0] == "f_pv" and t[2:] == (LPAIRS - 1, 1))
                        value.wait_filled(act, i, t0, "v", prev)
                        work.wait_filled(act, i, task, "v")
                        work.raise_read(a.activation(Vf[:, task[2], :, 0:HEAD], heads(work.bank(task, "v")), ACT.Copy), task, "v")
                    elif kind == "f_qkt":
                        t = task[2]
                        t0, prev = earlier(task, lambda t: t[0] == "f_down")
                        work.wait_filled(act, i, t0, "d", prev)
                        for m, dst in (("q", Qf), ("k", Kf)):
                            high(i, task, m, dst[0][:, :, t * P:(t + 1) * P],
                                 work.bank(task, m)[:, :].rearrange("p (c n) -> p c n", n=P))
                    elif kind == "f_ot":
                        high(i, task, "o", OfT[0][:, task[2], :], work.bank(task, "o")[:, :])
                    elif kind == "f_ln":
                        work.wait_read(act, i, task, "h")
                        a.activation(hT[0][:, :], ln_tmp, ACT.Copy).then_inc(hi_ready.sem, 1)
                    elif kind == "f_up":
                        _, l, j = task
                        m = HID_CHUNKS[j][1]
                        if j > 0:
                            work.wait_read(act, i, ("f_up", l, j - 1), "a")
                        work.wait_filled(act, i, task, "g")
                        work.raise_read(a.activation(gate[0:m, :], work.bank(task, "g")[0:m, :], ACT.Gelu,
                                                     bias=b1s[0:m, l, 1, j:j + 1]), task, "g")
                        work.wait_read(act, i, task, "a")
                        a.activation(GLU[0][0:m, j, :], glu[0:m, :], ACT.Copy).then_inc(hi_ready.sem, 1)

        @block.vector
        def _(dve):
            v = nc.vector
            for sig in own["dve"]:
                dve.sem_inc(sig.sem, sig.count)
            for r in (work, maxima, score, value):
                for slot, per in enumerate(r.per_slot):
                    dve.sem_inc(r.read[slot], per)
            dve.wait_ge(params, PARAMS)
            for l in range(DEPTH):
                for kind in range(4):
                    v.tensor_tensor(rope_t[:, l, kind], rope_t[:, l, kind],
                                    scales[:, l, kind:kind + 1, :].broadcast_to([P, TILES, HEAD]), ALU.mult).then_inc(tables, 1)
            for k, (_, rows, n, parts) in enumerate(pieces):
                dve.wait_ge(staged[k % 4], 16 * (k // 4 + 1))
                dve.wait_ge(split_hi, k + 1)
                v.tensor_tensor(parts[1], scratch[0:rows, k % 4, 0:n], parts[0].bitcast(F32), ALU.subtract).then_inc(split_lo, 1)
            dve.wait_ge(tables, 4 * DEPTH)
            dve.wait_ge(split_lo, len(pieces))
            dve.wait_ge(consts, CONSTS)

            def low(i, task, mark, dst, src, hi):
                dve.wait_ge(hi_ready.sem, hi_ready.now(i, task, mark))
                work.raise_read(v.tensor_tensor(dst, src, hi.bitcast(F32), ALU.subtract), task, mark)

            def low_biased(i, task, mark, dst, bias, hi):
                dve.wait_ge(hi_ready.sem, hi_ready.now(i, task, mark))
                work.raise_read(v.scalar_tensor_tensor(dst, work.bank(task, mark)[:, :], bias, hi.bitcast(F32),
                                                       ALU.add, ALU.subtract), task, mark)

            def token_norm(i, task, src):
                for t in range(TILES):
                    ins = v.bn_stats(stats[:, t, :], src[:, t, :])
                ins.then_inc(norm_ready.sem, 1)
                dve.wait_ge(norm_ready.sem, norm_ready.now(i, task, "s"))
                dve.sem_inc(carried["dve"], 1)
                for t in range(TILES):
                    ins = v.bn_aggr(mv[:, t, :], stats[:, t, :])
                ins.then_inc(norm_ready.sem, 1)
                dve.wait_ge(norm_ready.sem, norm_ready.now(i, task, "a"))
                v.tensor_scalar(var_eps[:, :], mv[:, :, 1], EPS, None, ALU.add).then_inc(norm_ready.sem, 1)
                dve.wait_ge(rstd_ready.sem, rstd_ready.now(i, task, "p"))
                for t in range(TILES):
                    ins = v.tensor_scalar(h[:, t, :], src[:, t, :], mv[:, t, 0:1], rstd[:, t:t + 1],
                                          ALU.subtract, ALU.mult)
                ins.then_inc(norm_ready.sem, 1)

            with dve.Fori(0, BATCH) as i:
                for task in SCHEDULE:
                    kind = task[0]
                    if kind == "in":
                        dve.wait_ge(x_loaded, 16 * i + 16)
                        work.wait_filled(dve, i, ("f_ln", DEPTH - 1), "h", True)
                        token_norm(i, task, x_in)
                        low(i, task, "x", xT[1][:, :], work.bank(task, "x")[:, :], xT[0][:, :])
                    elif kind == "a_proj":
                        p = task[1]
                        for c, (m, dst) in enumerate((("q", Qa), ("k", Ka))):
                            low_biased(i, task, m, dst[p % 2][1][:, :], bqkv[:, c * PAIRS + p:c * PAIRS + p + 1],
                                       dst[p % 2][0][:, :])
                        t0, prev = earlier(task, lambda t: t[0] == "a_pv" and t[1] % 2 == p % 2 and t[2] == 1)
                        value.wait_filled(dve, i, t0, "v", prev)
                        work.wait_filled(dve, i, task, "v")
                        work.raise_read(v.tensor_copy(
                            Va[p % 2][:, :, :, 0:HEAD],
                            work.bank(task, "v")[:, :].rearrange("p (t j d) -> p t j d", t=TILES, j=2)), task, "v")
                    elif kind == "a_max":
                        p = task[1]
                        t0, prev = earlier(task, lambda t: t[0] == "a_neg" and t[1] % 2 == p % 2)
                        work.wait_filled(dve, i, t0, "m", prev)
                        for j in range(2):
                            for u, parts in enumerate(MAX_USES):
                                maxima.wait_filled(dve, i, task, (j, u))
                                for t, at in parts:
                                    ins = v.tensor_reduce(neg[p % 2][:, t, j:j + 1],
                                                          maxima.bank(task, (j, u))[:, at:at + (t + 1) * P],
                                                          AX.X, ALU.max, negate=True)
                                maxima.raise_read(ins, task, (j, u))
                    elif kind == "f_max":
                        p = task[2]
                        t0, prev = earlier(task, lambda t: t[0] == "f_neg" and t[2] % 2 == p % 2)
                        work.wait_filled(dve, i, t0, "m", prev)
                        for j in range(2):
                            for u in range(2):
                                maxima.wait_filled(dve, i, task, (j, u))
                                maxima.raise_read(v.tensor_reduce(
                                    negf[p % 2][:, 2 * u:2 * u + 2, j],
                                    maxima.bank(task, (j, u))[:, 0:2 * BAND].rearrange("p (t n) -> p t n", t=2),
                                    AX.X, ALU.max, negate=True), task, (j, u))
                    elif kind in ("a_pv", "f_pv"):
                        j = task[-1]
                        rec, dst, ot = (rec_a, Oa, "a_ot") if kind == "a_pv" else (rec_f, Of, "f_ot")
                        bank = tiles_of(value.bank(task, "v")[:, 0:TILES * (HEAD + 1)])
                        value.wait_filled(dve, i, task, "v")
                        v.reciprocal(rec[:, :], bank[:, :, HEAD]).then_inc(rec_ready.sem, 1)
                        if j == 0:
                            t0, prev = earlier(task, lambda t: t[0] == ot)
                            work.wait_filled(dve, i, t0, "o", prev)
                            if task == ("a_pv", 0, 0):
                                work.wait_filled(dve, i, ("out",), "t", True)
                        dve.wait_ge(rec_ready.sem, rec_ready.now(i, task, "r"))
                        value.raise_read(v.tensor_tensor(dst[:, :, j * HEAD:(j + 1) * HEAD], bank[:, :, 0:HEAD],
                                                         rec[:, :].unsqueeze(2).broadcast_to([P, TILES, HEAD]), ALU.mult),
                                         task, "v")
                    elif kind == "a_ot":
                        p = task[1]
                        low_biased(i, task, "o", OaT[1][:, :], bqkv[:, 2 * PAIRS + p:2 * PAIRS + p + 1], OaT[0][:, :])
                    elif kind == "f_ht":
                        low(i, task, "h", hT[1][:, :], work.bank(task, "h")[:, :], hT[0][:, :])
                    elif kind == "f_qk":
                        _, l, t = task
                        hh = HEAD // 2
                        for s, c in enumerate("qk"):
                            dve.wait_ge(squares_ready.sem, squares_ready.now(i, task, c))
                            src = heads(work.bank(task, c))

                            def table(term, a, b):
                                return rope_t[:, l, 2 * s + term, t, a:b].unsqueeze(1).broadcast_to([P, LHEADS, b - a])

                            if s == 1:
                                dve.wait_ge(turned_ready.sem, turned_ready.now(i, task, "q"))
                            elif t > 0:
                                dve.wait_ge(turned_ready.sem, turned_ready.now(i, ("f_qk", l, t - 1), "k"))
                            elif l > 0:
                                dve.wait_ge(lo_ready.sem, lo_ready.now(i, ("f_up", l - 1, LAST_UP), "g"))
                            else:
                                dve.wait_ge(sum_ready.sem, sum_ready.before(i, ("out",), "o"))
                            if s == 0 and t == 0:
                                t0, prev = earlier(task, lambda t: t[0] == "f_up" and t[2] == LAST_UP)
                                dve.wait_ge(hi_ready.sem, (hi_ready.before if prev else hi_ready.now)(i, t0, "g"))
                            v.tensor_tensor(heads(turn_a), src, table(0, 0, HEAD), ALU.mult)
                            tb = heads(turn_b)
                            v.tensor_tensor(tb[:, :, 0:hh], src[:, :, hh:HEAD], table(1, 0, hh), ALU.mult)
                            v.tensor_tensor(tb[:, :, hh:HEAD], src[:, :, 0:hh], table(1, hh, HEAD), ALU.mult).then_inc(turn_ready.sem, 1)
                            work.raise_read(v.tensor_reduce(ss[:, :], heads(squares), AX.X, ALU.add), task, c)
                            work.wait_read(dve, i, task, c)
                            v.tensor_scalar(ssc[s][:, :], ss[:, :], 1e-24, None, ALU.max).then_inc(clip_ready.sem, 1)
                    elif kind == "f_qkt":
                        t = task[2]
                        for m, dst in (("q", Qf), ("k", Kf)):
                            low(i, task, m, dst[1][:, :, t * P:(t + 1) * P],
                                work.bank(task, m)[:, :].rearrange("p (c n) -> p c n", n=P), dst[0][:, :, t * P:(t + 1) * P])
                    elif kind == "f_ot":
                        low(i, task, "o", OfT[1][:, task[2], :], work.bank(task, "o")[:, :], OfT[0][:, task[2], :])
                    elif kind in ("f_wo", "f_down"):
                        m = "w" if kind == "f_wo" else "d"
                        if kind == "f_down":
                            dve.wait_ge(bias_ready.sem, bias_ready.now(i, ("f_ln", task[1]), "b"))
                        else:
                            dve.wait_ge(shifted, shifts_done(i, ("f_ht", task[1])))
                        work.wait_filled(dve, i, task, m)
                        work.raise_read(v.tensor_tensor(xl[:, :, :], tiles_of(work.bank(task, m)), xl[:, :, :], ALU.add), task, m)
                    elif kind == "f_ln":
                        l = task[1]
                        dve.wait_ge(shifted, shifts_done(i, task))
                        token_norm(i, task, h)
                        work.wait_filled(dve, i, task, "h")
                        work.raise_read(v.tensor_scalar(ln_tmp, work.bank(task, "h")[:, :], lng[:, l:l + 1],
                                                        lnb[:, l:l + 1], ALU.mult, ALU.add), task, "h")
                        dve.wait_ge(hi_ready.sem, hi_ready.now(i, task, "h"))
                        v.tensor_tensor(hT[1][:, :], ln_tmp, hT[0][:, :].bitcast(F32), ALU.subtract).then_inc(lo_ready.sem, 1)
                    elif kind == "f_up":
                        _, l, j = task
                        m = HID_CHUNKS[j][1]
                        if j > 0:
                            dve.wait_ge(hi_ready.sem, hi_ready.now(i, ("f_up", l, j - 1), "g"))
                            dve.wait_ge(lo_ready.sem, lo_ready.now(i, ("f_up", l, j - 1), "g"))
                        work.wait_read(dve, i, task, "g")
                        work.wait_filled(dve, i, task, "a")
                        work.raise_read(v.scalar_tensor_tensor(glu[0:m, :], work.bank(task, "a")[0:m, :], b1s[0:m, l, 0, j:j + 1],
                                                               gate[0:m, :], ALU.add, ALU.mult), task, "a")
                        dve.wait_ge(hi_ready.sem, hi_ready.now(i, task, "g"))
                        v.tensor_tensor(GLU[1][0:m, j, :], glu[0:m, :], GLU[0][0:m, j, :].bitcast(F32), ALU.subtract).then_inc(lo_ready.sem, 1)
                    elif kind == "out":
                        dve.wait_ge(out_ready.sem, out_ready.now(i, ("a_out", PAIRS - 1), "a"))
                        v.tensor_scalar(aT, out_acc[:, :], bout[:, 0:1], None, ALU.add).then_inc(aT_ready.sem, 1)
                        work.wait_filled(dve, i, task, "t")
                        work.raise_read(v.tensor_tensor(out_a, tiles_of(work.bank(task, "t")), xl[:, :, :], ALU.add), task, "t")

        @block.tensor
        def _(pe):
            mm = nc.tensor.matmul
            for sig in own["pe"]:
                pe.sem_inc(sig.sem, sig.count)
            for r in (work, maxima, score, value):
                for slot, per in enumerate(r.per_slot):
                    pe.sem_inc(r.filled[slot], per)
            pe.wait_ge(consts, CONSTS)
            pe.wait_ge(split_lo, len(pieces))

            def product(dst, left, right, first=True, last=True):
                mm(dst, left[0], right[0], start=first, stop=False)
                mm(dst, left[1], right[0], start=False, stop=False)
                return mm(dst, left[0], right[1], start=False, stop=last)

            def parts(pair, *index):
                return [t[index] for t in pair]

            def transposes(i, task, mark, src):
                bank = work.claim(pe, i, task, mark)
                for t in range(TILES):
                    ins = nc.tensor.transpose(bank[:, t * P:(t + 1) * P], src(t), ident[:, :])
                work.raise_filled(ins, task, mark)

            def wait_parts(i, task, mark):
                pe.wait_ge(hi_ready.sem, hi_ready.now(i, task, mark))
                if (task, mark) in lo_ready.at:
                    pe.wait_ge(lo_ready.sem, lo_ready.now(i, task, mark))
                else:
                    work.wait_read(pe, i, task, mark)

            ALLP = slice(0, P)

            def tile(t):
                return slice(t * P, (t + 1) * P)

            with pe.Fori(0, BATCH) as i:
                for task in SCHEDULE:
                    kind = task[0]
                    if kind == "in":
                        pe.wait_ge(norm_ready.sem, norm_ready.now(i, task, "n"))
                        transposes(i, task, "x", lambda t: h[:, t, :])
                    elif kind == "a_proj":
                        p = task[1]
                        if p == 0:
                            wait_parts(i, ("in",), "x")
                        for c, m in enumerate("qk"):
                            bank = work.claim(pe, i, task, m)
                            cols = slice(c * HEADS * HEAD + p * P, c * HEADS * HEAD + (p + 1) * P)
                            work.raise_filled(product(bank[:, :], parts(Wqkv, ALLP, cols), parts(xT, ALLP)), task, m)
                        bank = work.claim(pe, i, task, "v")
                        cols = slice(2 * HEADS * HEAD + p * P, 2 * HEADS * HEAD + (p + 1) * P)
                        for t in range(TILES):
                            ins = product(bank[:, tile(t)], parts(xT, ALLP, tile(t)), parts(Wqkv, ALLP, cols))
                        work.raise_filled(ins, task, "v")
                    elif kind == "a_max":
                        p = task[1]
                        pe.wait_ge(hi_ready.sem, hi_ready.now(i, ("a_proj", p), "k"))
                        Q, K = Qa[p % 2][0], Ka[p % 2][0]
                        for j in range(2):
                            rows = slice(j * HEAD, (j + 1) * HEAD)
                            for u, uses in enumerate(MAX_USES):
                                bank = maxima.claim(pe, i, task, (j, u))
                                for t, at in uses:
                                    n = (t + 1) * P
                                    mm(bank[:, at:at + n], Q[rows, tile(t)], K[rows, 0:n], start=True, stop=False)
                                    ins = mm(bank[:, at + n - P:at + n], mask_row[:, :], future_q[:, :], start=False, stop=True)
                                maxima.raise_filled(ins, task, (j, u))
                    elif kind == "f_max":
                        _, l, p = task
                        if p == 0:
                            pe.wait_ge(hi_ready.sem, hi_ready.now(i, ("f_qkt", l, TILES - 1), "k"))
                        for j in range(2):
                            rows = slice(j * HEAD, (j + 1) * HEAD)
                            for u in range(2):
                                bank = maxima.claim(pe, i, task, (j, u))
                                mm(bank[:, 0:2 * BAND], mask_row[:, :], band[:, u:u + 2, :].rearrange("p a n -> p (a n)"),
                                   start=True, stop=False)
                                for k in range(2):
                                    t = 2 * u + k
                                    k0 = t * P - WINDOW if t else 0
                                    at = k * BAND + (0 if t else WINDOW)
                                    ins = mm(bank[:, at:(k + 1) * BAND], Qf[0][rows, p, tile(t)],
                                             Kf[0][rows, p, k0:(t + 1) * P], start=False, stop=(k == 1))
                                maxima.raise_filled(ins, task, (j, u))
                    elif kind in ("a_neg", "f_neg"):
                        src, other, u = (neg, "a_max", 2) if kind == "a_neg" else (negf, "f_max", 1)
                        maxima.wait_all_read(pe, i, [((other, *task[1:]), (1, k)) for k in range(u + 1)])
                        bank = work.claim(pe, i, task, "m")[0:2, :].bitcast(BF16)
                        for t in range(TILES):
                            ins = nc.tensor.transpose(bank[:, tile(t)], src[task[-1] % 2][:, t, :], identb[:, :])
                        work.raise_filled(ins, task, "m")
                    elif kind == "a_st":
                        p, j = task[1], task[2]
                        rows = slice(j * HEAD, (j + 1) * HEAD)
                        if j == 0:
                            work.wait_all_read(pe, i, [(("a_proj", p), m) for m in "qk"])
                            work.wait_read(pe, i, ("a_neg", p), "m")
                        for u, (_, _, uses) in enumerate(CAUSAL_USES):
                            bank = score.claim(pe, i, task, u)
                            for k, at in uses:
                                n = SEQ - k * P
                                queries = slice(k * P, SEQ)
                                product(bank[:, at:at + n], parts(Ka[p % 2], rows, tile(k)), parts(Qa[p % 2], rows, queries), last=False)
                                mm(bank[:, at:at + n], pick[:, j, :], negT[p % 2][:, queries], start=False, stop=False)
                                ins = mm(bank[:, at:at + P], mask_row[:, :], future_k[:, :], start=False, stop=True)
                            score.raise_filled(ins, task, u)
                    elif kind == "f_st":
                        _, l, p, j = task
                        rows = slice(j * HEAD, (j + 1) * HEAD)
                        if j == 0:
                            if p == 0:
                                work.wait_all_read(pe, i, [(("f_qkt", l, t), m) for t in range(TILES) for m in "qk"])
                            work.wait_read(pe, i, ("f_neg", l, p), "m")
                        for u in range(2):
                            bank = score.claim(pe, i, task, u)
                            total = 2 * BAND if u == 0 else BAND + P
                            mm(bank[:, 0:total], mask_row[:, :], band[:, 1:3, :].rearrange("p a n -> p (a n)")[:, 0:total],
                               start=True, stop=False)
                            for k in range(2):
                                t = 2 * u + k
                                n = min(BAND, SEQ - t * P)
                                dst = bank[:, k * BAND:k * BAND + n]
                                queries = slice(t * P, t * P + n)
                                product(dst, parts(Kf, rows, p, tile(t)), parts(Qf, rows, p, queries), first=False, last=False)
                                ins = mm(dst, pick[:, j, :], negfT[p % 2][:, queries], start=False, stop=(k == 1))
                            score.raise_filled(ins, task, u)
                    elif kind == "a_pv":
                        p, j = task[1], task[2]
                        work.wait_read(pe, i, ("a_proj", p), "v")
                        score.wait_all_read(pe, i, [(("a_st", p, j), u) for u in range(3)])
                        bank = value.claim(pe, i, task, "v")
                        for t in range(TILES):
                            for k in range(t + 1):
                                at = CAUSAL_AT[k] + (t - k) * P
                                ins = mm(bank[:, t * (HEAD + 1):(t + 1) * (HEAD + 1)], probs[j][:, at:at + P],
                                         Va[p % 2][:, k, j, :], start=(k == 0), stop=(k == t))
                        value.raise_filled(ins, task, "v")
                    elif kind == "f_pv":
                        _, l, p, j = task
                        if p == 0 and j == 0:
                            work.wait_all_read(pe, i, [(("f_v", l, t), "v") for t in range(TILES)])
                        score.wait_all_read(pe, i, [(("f_st", l, p, j), u) for u in range(2)])
                        bank = value.claim(pe, i, task, "v")
                        for t in range(TILES):
                            to = bank[:, t * (HEAD + 1):(t + 1) * (HEAD + 1)]
                            ins = mm(to, lprobs[j][:, t * BAND:t * BAND + P], Vf[:, t, 2 * p + j, :], start=True, stop=True)
                            if t > 0:
                                ins = mm(to[0:WINDOW], lprobs[j][:, t * BAND - WINDOW:t * BAND], Vf[:, t - 1, 2 * p + j, :],
                                         start=False, stop=True, skip_group_check=True)
                        value.raise_filled(ins, task, "v")
                    elif kind == "a_ot":
                        value.wait_read(pe, i, ("a_pv", task[1], 1), "v")
                        transposes(i, task, "o", lambda t: Oa[:, t, :])
                    elif kind == "f_ot":
                        value.wait_read(pe, i, ("f_pv", task[1], task[2], 1), "v")
                        transposes(i, task, "o", lambda t: Of[:, t, :])
                    elif kind == "a_out":
                        p = task[1]
                        wait_parts(i, ("a_ot", p), "o")
                        if p == 0:
                            pe.wait_ge(aT_ready.sem, aT_ready.before(i, ("out",), "a"))
                        product(out_acc[:, :], parts(Wout, ALLP, p), parts(OaT, ALLP), first=(p == 0),
                                last=(p == PAIRS - 1)).then_inc(out_ready.sem, 1)
                    elif kind == "f_ht":
                        pe.wait_ge(shifted, shifts_done(i, task))
                        pe.wait_ge(zeroed, i * (16 * DEPTH) + 16 * (task[1] + 1))
                        transposes(i, task, "h", lambda t: h[:, t, :])
                    elif kind == "f_qk":
                        _, l, t = task
                        if t == 0:
                            wait_parts(i, ("f_ht", l), "h")
                        for c, m in enumerate("qk"):
                            bank = work.claim(pe, i, task, m)
                            work.raise_filled(product(bank[:, :], parts(hT, ALLP, tile(t)),
                                                      parts(Lqkv[l], ALLP, slice(c * INNER, (c + 1) * INNER))), task, m)
                    elif kind == "f_v":
                        _, l, t = task
                        bank = work.claim(pe, i, task, "v")
                        work.raise_filled(product(bank[:, :], parts(hT, ALLP, tile(t)),
                                                  parts(Lqkv[l], ALLP, slice(2 * INNER, 3 * INNER))), task, "v")
                    elif kind == "f_qkt":
                        _, l, t = task
                        for s, m in enumerate("qk"):
                            pe.wait_ge(qk_ready.sem, qk_ready.now(i, ("f_qk", l, t), m))
                            transposes(i, task, m, lambda c: qkn[s][:, tile(c)])
                    elif kind == "f_wo":
                        l = task[1]
                        wait_parts(i, ("f_ot", l, LPAIRS - 1), "o")
                        bank = work.claim(pe, i, task, "w")
                        for t in range(TILES):
                            for c in range(LPAIRS):
                                ins = product(bank[:, tile(t)], parts(OfT, ALLP, c, tile(t)), parts(Lwo[l], ALLP, c),
                                              first=(c == 0), last=(c == LPAIRS - 1))
                        work.raise_filled(ins, task, "w")
                    elif kind == "f_ln":
                        pe.wait_ge(norm_ready.sem, norm_ready.now(i, task, "n"))
                        transposes(i, task, "h", lambda t: h[:, t, :])
                    elif kind == "f_up":
                        _, l, j = task
                        c, m = HID_CHUNKS[j]
                        if j == 0:
                            wait_parts(i, ("f_ln", l), "h")
                        for half, mark in ((1, "g"), (0, "a")):
                            bank = work.claim(pe, i, task, mark)
                            at = half * HID + c
                            work.raise_filled(product(bank[0:m, :], parts(Lw1[l], ALLP, slice(at, at + m)), parts(hT, ALLP)),
                                              task, mark)
                    elif kind == "f_down":
                        l = task[1]
                        wait_parts(i, ("f_up", l, LAST_UP), "g")
                        bank = work.claim(pe, i, task, "d")
                        for t in range(TILES):
                            for j, (c, m) in enumerate(HID_CHUNKS):
                                ins = product(bank[:, tile(t)], parts(GLU, slice(0, m), j, tile(t)),
                                              parts(Lw2[l], slice(0, m), j), first=(j == 0), last=(j == LAST_UP))
                        work.raise_filled(ins, task, "d")
                    elif kind == "out":
                        pe.wait_ge(aT_ready.sem, aT_ready.now(i, task, "a"))
                        transposes(i, task, "t", lambda t: aT[:, tile(t)])


PARAMS = 16 * (4 + DEPTH * (2 * len(HID_CHUNKS) + 1 + 6 + 4))
CONSTS = 20

_INS = ["L0_attn_x", "L0_attn_W_qkv", "L0_attn_b_qkv", "L0_attn_W_out", "L0_attn_b_out", "L0_ffn_wqkv",
        "L0_ffn_q_scale", "L0_ffn_k_scale", "L0_ffn_wo", "L0_ffn_ln_g", "L0_ffn_ln_b", "L0_ffn_w1", "L0_ffn_b1",
        "L0_ffn_w2", "L0_ffn_b2"]


def kernel(**inputs):
    import numpy as _np
    import concourse.bacc as _bacc
    from concourse import mybir as _mybir
    from concourse.bass_utils import run_bass_kernel_spmd as _run

    nc = _bacc.Bacc("TRN2", target_bir_lowering=False, num_devices=1)
    arrays, args = {}, []
    for name in _INS:
        a = _np.ascontiguousarray(inputs[name])
        arrays[f"in_{name}"] = a
        args.append(nc.dram_tensor(f"in_{name}", a.shape, _mybir.dt.from_np(a.dtype), kind="ExternalInput").ap())
    rope = rope_tables()
    arrays["in_rope"] = rope
    args.append(nc.dram_tensor("in_rope", rope.shape, _mybir.dt.float32, kind="ExternalInput").ap())
    out = nc.dram_tensor("out_0", (BATCH, SEQ, DIM), _mybir.dt.float32, kind="ExternalOutput").ap()
    prenorm_attention_and_local_transformer(nc, *args, out)
    r = _run(nc, [arrays], core_ids=[0])
    return r.results[0]["out_0"]
```

```python
import numpy as np
from contextlib import ExitStack

import concourse.bass as bass
from concourse import mybir

F32 = mybir.dt.float32
F32R = mybir.dt.float32r
BF16 = mybir.dt.bfloat16
ALU = mybir.AluOpType
ACT = mybir.ActivationFunctionType
AX = mybir.AxisListType

BATCH, SEQ, DIM = 16, 512, 128
P = 128
TILES = SEQ // P
HEAD = 64
HEADS = 16
PAIRS = HEADS * HEAD // P
WINDOW = 64
DEPTH = 2
LHEADS = 8
LPAIRS = LHEADS * HEAD // P
INNER = LHEADS * HEAD
HID = int(DIM * 4 * 2 / 3)
HID_CHUNKS = [(c, min(P, HID - c)) for c in range(0, HID, P)]
BAND = P + WINDOW
QK_SCALE = 8.0
EPS = 1e-5
MASK_ROW = 16000.0
MASK_CAUSAL = -5.0
MASK_BAND = -float(2.0 ** 110)
CAUSAL_AT = [0, 512, 1024, 896]
CAUSAL_USES = [(0, 512, [(0, 0)]), (512, 512, [(1, 0), (3, 384)]), (1024, 256, [(2, 0)])]
MAX_USES = [[(0, 0), (1, P)], [(2, 0)], [(3, 0)]]


A_ROUND = [("a_proj", 1), ("a_max", 1), ("a_st", 0, 0), ("a_ot", -1), ("a_st", 0, 1), ("a_pv", 0, 0),
           ("a_out", -1), ("a_neg", 1), ("a_pv", 0, 1)]
F_ROUND = [("f_st", 0, 0), ("f_max", 1), ("f_ot", -1), ("f_st", 0, 1), ("f_neg", 1), ("f_pv", 0, 0),
           ("f_pv", 0, 1)]
F_FRONT = [("f_qk", 0), ("f_v", 0), ("f_qk", 1), ("f_qkt", 0), ("f_v", 1), ("f_qk", 2), ("f_v", 2),
           ("f_qkt", 1), ("f_qk", 3), ("f_v", 3), ("f_qkt", 2), ("f_qkt", 3)]
WEIGHT = {"a_proj": 2.0, "a_max": 1.5, "a_neg": 0.2, "a_st": 3.6, "a_ot": 0.5, "a_pv": 1.1, "a_out": 0.7,
          "a_end": 0.2, "f_ht": 5.0, "f_qk": 3.0, "f_v": 1.0, "f_qkt": 2.0, "f_max": 1.5, "f_neg": 0.7,
          "f_st": 1.5, "f_ot": 1.0, "f_pv": 1.0, "f_wo": 3.0, "f_wot": 2.55, "f_norm": 3.5, "f_ln": 2.0,
          "norm": 1.0, "f_up": 1.5, "f_split": 1.5, "xt": 1.0, "f_down": 3.0, "f_downt": 3.0}


def rounds(steps, pairs, layer=()):
    return [(step[0], *layer, r + step[1], *step[2:]) for r in range(-1, pairs + 1) for step in steps
            if 0 <= r + step[1] < pairs]


def attention_tasks():
    return rounds(A_ROUND, PAIRS) + [("a_end",)]


def local_tasks(l):
    out = [("f_ht", l)] + [(kind, l, t) for kind, t in F_FRONT] + rounds(F_ROUND, LPAIRS, (l,))
    out += [("f_wo", l), ("f_wot", l), ("f_norm", l), ("f_ln", l)]
    out += [("norm",)] if l == DEPTH - 1 else []
    for j in range(len(HID_CHUNKS)):
        out += [("f_up", l, j)] + ([("f_split", l, j - 1)] if j else [])
    out += [("f_split", l, len(HID_CHUNKS) - 1)]
    out += [("xt",)] if l == DEPTH - 1 else []
    return out + [("f_down", l), ("f_downt", l)]


def merged(a, b):
    total = [sum(WEIGHT[task[0]] for task in part) for part in (a, b)]
    out, n, spent = [], [0, 0], [0.0, 0.0]
    while n[0] < len(a) or n[1] < len(b):
        side = 0 if n[1] >= len(b) or (n[0] < len(a) and spent[0] / total[0] <= spent[1] / total[1]) else 1
        task = (a, b)[side][n[side]]
        out.append(task)
        n[side] += 1
        spent[side] += WEIGHT[task[0]]
    return out


SCHEDULE = merged(attention_tasks(), local_tasks(0) + local_tasks(1)) + [("out",), ("start",)]
AHEAD = ("norm", "xt", "start")
assert SCHEDULE.index(("xt",)) > SCHEDULE.index(("a_proj", PAIRS - 1))


def earlier(task, which):
    at = SCHEDULE.index(task)
    for k in range(at - 1, at - 1 - len(SCHEDULE), -1):
        if which(SCHEDULE[k]):
            return SCHEDULE[k], k < 0
    raise ValueError(task)


class Signal:

    def __init__(self, sem, marks):
        self.sem = sem
        self.names = [(task, m) for task in SCHEDULE for m in marks.get(task[0], ())]
        self.at = {n: k + 1 for k, n in enumerate(self.names)}
        self.count = len(self.names)

    def sems(self, task):
        return [(self.sem, sum(n[0] == task for n in self.names))]

    def now(self, i, task, mark):
        return i * self.count + (self.count + self.at[task, mark])

    def before(self, i, task, mark):
        return i * self.count + self.at[task, mark]


class Ring:

    def __init__(self, banks, filled, read, marks):
        self.banks, self.filled, self.read = banks, filled, read
        n = len(banks)
        self.use = {}
        self.per_slot = [0] * n
        k = 0
        for task in SCHEDULE:
            for m in marks.get(task[0], ()):
                self.per_slot[k % n] += 1
                self.use[task, m] = (k % n, self.per_slot[k % n])
                k += 1

    def sems(self, task, which):
        return [(which[slot], 1) for (t, _), (slot, _) in self.use.items() if t == task]

    def bank(self, task, mark):
        return self.banks[self.use[task, mark][0]]

    def wait_filled(self, engine, i, task, mark, before=False):
        slot, k = self.use[task, mark]
        per = self.per_slot[slot]
        engine.wait_ge(self.filled[slot], i * per + (k if before else per + k))

    def wait_read(self, engine, i, task, mark, before=False):
        slot, k = self.use[task, mark]
        per = self.per_slot[slot]
        engine.wait_ge(self.read[slot], i * per + (k if before else per + k))

    def wait_all_read(self, engine, i, uses):
        last = {self.use[u][0]: u for u in sorted(uses, key=lambda u: self.use[u][1])}
        for task, mark in last.values():
            self.wait_read(engine, i, task, mark)

    def claim(self, engine, i, task, mark, after=()):
        slot, k = self.use[task, mark]
        last = {slot: k - 1}
        for u in after:
            last[self.use[u][0]] = max(self.use[u][1], last.get(self.use[u][0], 0))
        for other, n in last.items():
            if isinstance(i, int) and (i + 1) * self.per_slot[other] + n == 0:
                continue
            engine.wait_ge(self.read[other], i * self.per_slot[other] + (self.per_slot[other] + n))
        return self.banks[slot]

    def raise_filled(self, ins, task, mark):
        ins.then_inc(self.filled[self.use[task, mark][0]], 1)

    def raise_read(self, ins, task, mark):
        ins.then_inc(self.read[self.use[task, mark][0]], 1)


def before_first(engine, ordered, sems_of, steps):
    counts, reached = {}, {}

    def raise_counts():
        for sem, n in counts.values():
            engine.sem_inc(sem, n)
        counts.clear()

    for task in SCHEDULE:
        if task[0] in AHEAD:
            raise_counts()
            steps(-1, [task])
        for sem, n in sems_of(task):
            if n:
                reached[id(sem)] = reached.get(id(sem), 0) + n
                if task[0] in AHEAD:
                    engine.wait_ge(sem, reached[id(sem)])
                    engine.sem_inc(ordered, 1)
                else:
                    counts[id(sem)] = (sem, counts.get(id(sem), (sem, 0))[1] + n)
    raise_counts()


def rope_tables():
    half = np.arange(0, HEAD, 2, dtype=np.float32)
    inv_freq = (np.float32(1.0) / np.float32(10000.0) ** (half / np.float32(HEAD))).astype(np.float32)
    t = np.arange(SEQ, dtype=np.float32)
    freqs = t[:, None] * inv_freq[None, :]
    freqs = np.concatenate([freqs, freqs], axis=-1)
    base = (half + np.float32(0.4 * HEAD)) / np.float32(1.4 * HEAD)
    power = (t - np.float32(SEQ // 2)) / np.float32(WINDOW // 2)
    scale = base[None, :] ** power[:, None]
    scale = np.concatenate([scale, scale], axis=-1)
    cos, sin = np.cos(freqs), np.sin(freqs)
    sign = np.concatenate([-np.ones(HEAD // 2), np.ones(HEAD // 2)]).astype(np.float32)[None, :]
    out = np.stack([cos * scale * np.float32(QK_SCALE), sin * sign * scale * np.float32(QK_SCALE),
                    cos / scale, sin * sign / scale])
    return out.astype(np.float32)


def prenorm_attention_and_local_transformer(nc, x, W_qkv, b_qkv, W_out, b_out, wqkv, q_scale, k_scale,
                                            wo, ln_g, ln_b, w1, b1, w2, b2, rope, out):
    ctx = ExitStack()
    with ctx:
        def sb(name, shape, dt=F32):
            return ctx.enter_context(nc.sbuf_tensor(name, shape, dt))

        def sem(name):
            return ctx.enter_context(nc.semaphore(name))

        Wqkv = [sb(f"Wqkv_{s}", [P, 3 * HEADS * HEAD], F32R) for s in ("hi", "lo")]
        Wout = [sb(f"Wout_{s}", [P, PAIRS, DIM], F32R) for s in ("hi", "lo")]
        Lqkv = [[sb(f"Lqkv{l}_{s}", [P, 3 * INNER], F32R) for s in ("hi", "lo")] for l in range(DEPTH)]
        Lwo = [[sb(f"Lwo{l}_{s}", [P, LPAIRS, DIM], F32R) for s in ("hi", "lo")] for l in range(DEPTH)]
        Lw1 = [[sb(f"Lw1{l}_{s}", [P, 2 * HID], F32R) for s in ("hi", "lo")] for l in range(DEPTH)]
        Lw2 = [[sb(f"Lw2{l}_{s}", [P, len(HID_CHUNKS), DIM], F32R) for s in ("hi", "lo")] for l in range(DEPTH)]
        bqkv = sb("bqkv", [P, 3 * PAIRS])
        bout = sb("bout", [P, 1])
        lng, lnb = sb("lng", [P, DEPTH]), sb("lnb", [P, DEPTH])
        b1s = sb("b1s", [P, DEPTH, 2, len(HID_CHUNKS)])
        b2s = sb("b2s", [P, DEPTH])
        rope_t = sb("rope_t", [P, DEPTH, 4, TILES, HEAD])

        ident = sb("ident", [P, P])
        identb = sb("identb", [P, P], BF16)
        mask_row = sb("mask_row", [P, P], BF16)
        future_q = sb("future_q", [P, P], BF16)
        future_k = sb("future_k", [P, P], BF16)
        band = sb("band", [P, 3, BAND], BF16)
        pick = sb("pick", [2, 2, P], BF16)
        minus_half = sb("minus_half", [P, LHEADS])
        zero_row = sb("zero_row", [1, DIM // 2])

        x_res = sb("x_res", [P, TILES, DIM])
        xl = sb("xl", [P, TILES, DIM])
        xT = [sb(f"xT_{s}", [P, SEQ], F32R) for s in ("hi", "lo")]
        h = sb("h", [P, TILES, DIM])
        hT = [sb(f"hT_{s}", [P, SEQ], F32R) for s in ("hi", "lo")]
        stats = sb("stats", [P, TILES, 6])
        mv = sb("mv", [P, TILES, 2])
        var_eps = sb("var_eps", [P, TILES])
        rstd = sb("rstd", [P, TILES])
        Qa = [[sb(f"Qa{b}_hi", [P, 2, SEQ], F32R), sb(f"Qa{b}_lo", [P, SEQ], F32R)] for b in range(2)]
        Ka = [[sb(f"Ka{b}_{s}", [P, SEQ], F32R) for s in ("hi", "lo")] for b in range(2)]
        Va = [sb(f"Va{b}", [P, TILES, 2, HEAD + 1]) for b in range(2)]
        neg = [sb(f"neg{b}", [P, TILES, 2], BF16) for b in range(2)]
        negT = [sb(f"negT{b}", [2, SEQ], BF16) for b in range(2)]
        probs = [sb(f"probs{b}", [P, 1280]) for b in range(2)]
        Oa = sb("Oa", [P, TILES, P])
        OaT = [sb(f"OaT_{s}", [P, SEQ], F32R) for s in ("hi", "lo")]
        rec_a = sb("rec_a", [P, TILES])
        aT = Oa[:, :, :].rearrange("p t n -> p (t n)")
        Qf = [sb(f"Qf_{s}", [P, LPAIRS, SEQ], F32R) for s in ("hi", "lo")]
        Kf = [sb(f"Kf_{s}", [P, LPAIRS, SEQ], F32R) for s in ("hi", "lo")]
        Vf = sb("Vf", [P, TILES, LHEADS, HEAD + 1])
        negf = [sb(f"negf{b}", [P, TILES, 2], BF16) for b in range(2)]
        negfT = [sb(f"negfT{b}", [2, SEQ], BF16) for b in range(2)]
        lprobs = [sb(f"lprobs{b}", [P, 4 * BAND - WINDOW]) for b in range(2)]
        scales = lprobs[0][:, 0:DEPTH * 4 * HEAD].rearrange("p (l k d) -> p l k d", l=DEPTH, k=4)
        Of = sb("Of", [P, TILES, P])
        rec_f = sb("rec_f", [P, TILES])
        scratch = sb("scratch", [P, 4, SEQ])
        qkn = [Of[:, :, :].rearrange("p t n -> p (t n)"), lprobs[1][:, 0:INNER]]
        ss = sb("ss", [P, LHEADS])
        ssc = [sb(f"ssc{s}", [P, LHEADS]) for s in range(2)]
        rnorm = [sb(f"rnorm{s}", [P, LHEADS]) for s in range(2)]
        squares, turn_a, turn_b, turned = (scratch[:, k] for k in range(4))
        ln_tmp = scratch[:, 3]
        gate, glu = [scratch[:, 0], scratch[:, 3]], [scratch[:, 1], scratch[:, 2]]
        out_a = scratch[:, 2].rearrange("p (t d) -> p t d", t=TILES)
        yT = scratch[:, 2]
        x_rows = scratch[:, 3].rearrange("p (t d) -> p t d", t=TILES)
        OfT, GLU = Qf, Kf

        banks = [ctx.enter_context(nc.psum_tensor(f"bank{k}", [P, 512], F32)) for k in range(8)]

        RING = 7
        psum = Ring(banks[0:RING], [sem(f"bank{k}_filled") for k in range(RING)],
                    [sem(f"bank{k}_read") for k in range(RING)], dict(
            a_proj="qkv", a_neg="m", a_ot="o", f_ht="h", f_qk="qk", f_v="v", f_qkt="qk", f_neg="m", f_ot="o",
            f_wo="w", f_wot="t", f_ln="h", f_up="ga", f_down="w", f_downt="t", out="t", xt="x",
            a_max=[(j, u) for j in range(2) for u in range(3)], f_max=[(j, u) for j in range(2) for u in range(2)],
            a_st=[0, 1, 2], f_st=[0, 1],
            a_pv="v", f_pv="v"))
        out_acc = banks[RING]

        hi_ready = Signal(sem("hi_ready"), dict(
            a_proj=[("q", 0), ("q", 1), "k"], a_ot="o", f_ht="h", f_qkt="qk", f_ot="o", f_ln="h", f_split="g",
            xt="x"))
        lo_ready = Signal(sem("lo_ready"), dict(f_ln="h", f_split="g"))
        squares_ready = Signal(sem("squares_ready"), dict(f_qk="qk"))
        rec_ready = Signal(sem("rec_ready"), dict(a_pv="r", f_pv="r"))
        turn_ready = Signal(sem("turn_ready"), dict(f_qk="qk"))
        clip_ready = Signal(sem("clip_ready"), dict(f_qk="qk"))
        norm_ready = Signal(sem("norm_ready"), dict(f_norm="saen", norm="saen"))
        rstd_ready = Signal(sem("rstd_ready"), dict(f_norm="p", norm="p"))
        rnorm_ready = Signal(sem("rnorm_ready"), dict(f_qk="qk"))
        turned_ready = {"q": Signal(sem("turned_q_ready"), dict(f_qk="q")), "k": Signal(sem("turned_k_ready"), dict(f_qk="k"))}
        qk_ready = Signal(sem("qk_ready"), dict(f_qk="qk"))
        copy_ready = Signal(sem("copy_ready"), dict(start="x"))
        sum_ready = Signal(sem("sum_ready"), dict(out="o"))
        out_ready = Signal(sem("out_ready"), dict(a_out="a"))
        aT_ready = Signal(sem("aT_ready"), dict(a_end="a"))
        own = {
            "act": [hi_ready, squares_ready],
            "dve": [lo_ready, rec_ready, turn_ready, clip_ready, norm_ready, aT_ready, turned_ready["q"]],
            "pool": [rstd_ready, rnorm_ready, turned_ready["k"], qk_ready, copy_ready, sum_ready],
            "pe": [out_ready]}
        x_loaded, x_again, shifted, stored, zeroed = (sem(name) for name in ("x_loaded", "x_again", "shifted", "stored", "zeroed"))
        staged = [sem(f"staged{k}") for k in range(4)]
        split_hi, split_lo = sem("split_hi"), sem("split_lo")
        carried = {engine: sem(f"carried_{engine}") for engine in ("sp", "pool", "dve", "pe", "act")}
        params, consts, tables = sem("params"), sem("consts"), sem("tables")

        pieces = []
        for c in range(0, 3 * HEADS * HEAD, 512):
            pieces.append((W_qkv[:, c:c + 512], P, 512, [w[:, c:c + 512] for w in Wqkv]))
        for c in range(0, PAIRS, 4):
            pieces.append((W_out[c * P:(c + 4) * P, :].rearrange("(c p) n -> p c n", p=P), P, 512,
                           [w[:, c:c + 4, :].rearrange("p c n -> p (c n)") for w in Wout]))
        for l in range(DEPTH):
            for c in range(0, 3 * INNER, 512):
                pieces.append((wqkv[l, :, c:c + 512], P, 512, [w[:, c:c + 512] for w in Lqkv[l]]))
            pieces.append((wo[l].rearrange("(c p) n -> p c n", p=P), P, 512,
                           [w[:, :, :].rearrange("p c n -> p (c n)") for w in Lwo[l]]))
            for c in range(0, 2 * HID, 512):
                n = min(512, 2 * HID - c)
                pieces.append((w1[l, :, c:c + n], P, n, [w[:, c:c + n] for w in Lw1[l]]))
            for j, (c, n) in enumerate(HID_CHUNKS):
                pieces.append((w2[l, c:c + n, :], n, DIM, [w[0:n, j, :] for w in Lw2[l]]))

        def stage(k):
            src, rows, n, _ = pieces[k]
            to = scratch[0:rows, k % 4, 0:n]
            return to.rearrange("p (c n) -> p c n", c=src.shape[1]) if len(src.shape) == 3 else to

        def shifts_done(i, task):
            return i * (3 * 16 * 2 * DEPTH) + 3 * 16 * (2 * task[1] + (2 if task[0] == "f_norm" else 1))

        LAST_UP = len(HID_CHUNKS) - 1
        heads = lambda ap: ap.rearrange("p (h d) -> p h d", d=HEAD)
        tiles_of = lambda ap: ap.rearrange("p (t n) -> p t n", t=TILES)

        block = ctx.enter_context(nc.Block())

        @block.sync
        def _(sp):
            count = 0

            def param(dst, src):
                nonlocal count
                sp.dma_start(dst, src, allow_slow_non_contiguous=True).then_inc(params, 16)
                count += 16

            param(bqkv[:, :], b_qkv.rearrange("(c p) -> p c", p=P))
            param(bout[:, :], b_out.rearrange("(p a) -> p a", a=1))
            param(lng[:, :], ln_g.rearrange("l p -> p l"))
            param(lnb[:, :], ln_b.rearrange("l p -> p l"))
            param(b2s[:, :], b2.rearrange("l p -> p l"))
            for l in range(DEPTH):
                for half in range(2):
                    for j, (c, m) in enumerate(HID_CHUNKS):
                        at = half * HID + c
                        param(b1s[0:m, l, half, j:j + 1], b1[l, at:at + m].rearrange("(p a) -> p a", a=1))
                hh = HEAD // 2
                for s, src in enumerate((q_scale, k_scale)):
                    param(scales[:, l, 2 * s, :], src[l:l + 1, :].broadcast_to([P, HEAD]))
                    param(scales[:, l, 2 * s + 1, 0:hh], src[l:l + 1, hh:HEAD].broadcast_to([P, hh]))
                    param(scales[:, l, 2 * s + 1, hh:HEAD], src[l:l + 1, 0:hh].broadcast_to([P, hh]))
                for kind in range(4):
                    param(rope_t[:, l, kind, :, :], rope[kind].rearrange("(t p) d -> p t d", p=P))
            assert count == PARAMS, count
            for k, (src, _, _, _) in enumerate(pieces):
                if k >= 4:
                    sp.wait_ge(split_lo, k - 3)
                sp.dma_start(stage(k), src).then_inc(staged[k % 4], 16)
            half = DIM // 2
            sp.sem_inc(stored, 16)
            def load(dst, row, done):
                sp.dma_start(dst, x[row].rearrange("a (t p) d -> p (a t) d", p=P)).then_inc(done, 16)

            load(x_res[:, :, :], slice(0, 1), x_loaded)

            def sequence(i, last):
                sp.wait_ge(norm_ready.sem, norm_ready.before(i, ("norm",), "n"))
                sp.sem_inc(carried["sp"], 1)
                if last:
                    sp.sem_inc(x_loaded, 16)
                else:
                    load(x_res[:, :, :], bass.ds(i + 1, 1), x_loaded)
                for task in SCHEDULE:
                    kind = task[0]
                    if kind in ("f_ht", "f_norm"):
                        if kind == "f_norm":
                            psum.wait_read(sp, i, ("f_wot", task[1]), "t")
                        elif task[1] > 0:
                            psum.wait_read(sp, i, ("f_downt", task[1] - 1), "t")
                        else:
                            sp.wait_ge(copy_ready.sem, copy_ready.before(i, ("start",), "x"))
                        sp.sem_inc(carried["sp"], 1)
                        t0, prev = earlier(task, lambda t: t[0] in ("f_ht", "f_ln", "xt"))
                        psum.wait_filled(sp, i, t0, "x" if t0[0] == "xt" else "h", prev)
                        sp.sem_inc(carried["sp"], 1)
                        sp.dma_start(h[:, :, 0:half], xl[:, :, 0:half]).then_inc(shifted, 16)
                        sp.dma_start(h[1:P, :, half:DIM], xl[0:P - 1, :, half:DIM]).then_inc(shifted, 16)
                        if kind == "f_ht":
                            sp.dma_start(h[0:1, 0, half:DIM], zero_row[:, :]).then_inc(zeroed, 16)
                        sp.dma_start(h[0:1, 1:TILES, half:DIM], xl[P - 1:P, 0:TILES - 1, half:DIM]).then_inc(shifted, 16)
                    elif task == ("f_split", DEPTH - 1, LAST_UP):
                        sp.wait_ge(lo_ready.sem, lo_ready.now(i, task, "g"))
                        sp.sem_inc(carried["sp"], 1)
                        load(x_rows, bass.ds(i, 1), x_again)
                    elif kind == "out":
                        sp.wait_ge(sum_ready.sem, sum_ready.now(i, task, "o"))
                        sp.sem_inc(carried["sp"], 1)
                        sp.dma_start(out[bass.ds(i, 1)].rearrange("a (t p) d -> p (a t) d", p=P), out_a).then_inc(stored, 16)

            with sp.Fori(0, BATCH - 1) as i:
                sequence(i, False)
            sequence(BATCH - 1, True)
            sp.wait_ge(stored, 16 * BATCH + 16)

        @block.gpsimd
        def _(pool):
            g = nc.gpsimd
            made = [0]

            def const(ins):
                made[0] += 1
                ins.then_inc(consts, 1)
                pool.wait_ge(consts, made[0])

            def select(m, compare, fill, base, pattern, by_row):
                const(g.affine_select(out=m, in_=m, compare_op=compare, fill=fill, base=base, pattern=pattern,
                                      channel_multiplier=by_row))

            const(g.memset(ident[:, :], 0.0))
            select(ident[:, :], ALU.not_equal, 1.0, 0, [[-1, P]], 1)
            const(g.tensor_copy(identb[:, :], ident[:, :]))
            const(g.memset(mask_row[:, :], 0.0))
            select(mask_row[:, :], ALU.not_equal, MASK_ROW, 0, [[-1, P]], 1)
            const(g.memset(future_q[:, :], 0.0))
            select(future_q[:, :], ALU.is_ge, MASK_CAUSAL, 0, [[-1, P]], 1)
            const(g.memset(future_k[:, :], 0.0))
            select(future_k[:, :], ALU.is_ge, MASK_CAUSAL, 0, [[1, P]], -1)
            const(g.memset(band[:, :, :], 0.0))
            const(g.memset(band[:, 0, 0:WINDOW], MASK_BAND))
            select(band[:, :, :], ALU.is_ge, MASK_BAND, 0, [[0, 3], [1, BAND]], -1)
            select(band[:, :, :], ALU.is_ge, MASK_BAND, WINDOW, [[0, 3], [-1, BAND]], 1)
            const(g.memset(pick[:, :, :], 0.0))
            select(pick[:, :, :], ALU.not_equal, 1.0, 0, [[-1, 2], [0, P]], 1)
            const(g.memset(minus_half[:, :], -0.5))
            for b in range(2):
                const(g.memset(Va[b][:, :, :, HEAD:HEAD + 1], 1.0))
            const(g.memset(Vf[:, :, :, HEAD:HEAD + 1], 1.0))
            const(g.memset(zero_row[:, :], 0.0))
            for b in range(2):
                const(g.memset(Qa[b][0][HEAD:P, 0, :].bitcast(F32), 0.0))
                const(g.memset(Qa[b][0][0:HEAD, 1, :].bitcast(F32), 0.0))
            assert made[0] == CONSTS, made[0]

            def steps(i, tasks):
                for task in tasks:
                    kind = task[0]
                    if kind in ("norm", "f_norm"):
                        pool.wait_ge(norm_ready.sem, norm_ready.now(i, task, "e"))
                        g.tensor_tensor(rstd[:, :], var_eps[:, :], minus_half[:, 0:TILES], ALU.pow).then_inc(rstd_ready.sem, 1)
                    elif kind == "start":
                        pool.wait_ge(norm_ready.sem, norm_ready.now(i, ("norm",), "n"))
                        psum.wait_read(pool, i, ("out",), "t")
                        pool.sem_inc(carried["pool"], 1)
                        g.tensor_copy(xl[:, :, :], h[:, :, :]).then_inc(copy_ready.sem, 1)
                    elif kind == "f_qk":
                        for s, c in enumerate("qk"):
                            if s == 1:
                                pool.wait_ge(qk_ready.sem, qk_ready.now(i, task, "q"))
                            else:
                                t0, prev = earlier(task, lambda t: t[0] == "f_qk")
                                pool.wait_ge(qk_ready.sem, (qk_ready.before if prev else qk_ready.now)(i, t0, "k"))
                            pool.wait_ge(clip_ready.sem, clip_ready.now(i, task, c))
                            g.tensor_tensor(rnorm[s][:, :], ssc[s][:, :], minus_half[:, :], ALU.pow).then_inc(rnorm_ready.sem, 1)
                            if c == "k":
                                pool.wait_ge(turn_ready.sem, turn_ready.now(i, task, c))
                                g.tensor_tensor(turned, turn_a, turn_b, ALU.add).then_inc(turned_ready[c].sem, 1)
                            pool.wait_ge(rnorm_ready.sem, rnorm_ready.now(i, task, c))
                            pool.wait_ge(turned_ready[c].sem, turned_ready[c].now(i, task, c))
                            if task[2] > 0:
                                psum.wait_filled(pool, i, ("f_qkt", task[1], task[2] - 1), c)
                            g.tensor_tensor(heads(qkn[s]), heads(turned),
                                            rnorm[s][:, :].unsqueeze(2).broadcast_to([P, LHEADS, HEAD]),
                                            ALU.mult).then_inc(qk_ready.sem, 1)
                    elif kind == "out":
                        psum.wait_read(pool, i, task, "t")
                        pool.wait_ge(x_again, 16 * i + 16)
                        g.tensor_tensor(out_a, x_rows, out_a, ALU.add).then_inc(sum_ready.sem, 1)

            before_first(pool, carried["pool"], lambda task: [e for sig in own["pool"] for e in sig.sems(task)], steps)
            with pool.Fori(0, BATCH) as i:
                steps(i, SCHEDULE)

        @block.scalar
        def _(act):
            a = nc.scalar
            act.wait_ge(params, PARAMS)
            for k, (_, rows, n, parts) in enumerate(pieces):
                act.wait_ge(staged[k % 4], 16 * (k // 4 + 1))
                a.activation(parts[0], scratch[0:rows, k % 4, 0:n], ACT.Copy).then_inc(split_hi, 1)
            act.wait_ge(split_lo, len(pieces))

            def high(i, task, mark, dst, src, func=ACT.Copy, **kw):
                psum.wait_filled(act, i, task, mark[0])
                a.activation(dst, src, func, **kw).then_inc(hi_ready.sem, 1)

            def steps(i, tasks):
                for task in tasks:
                    kind = task[0]
                    if kind == "xt":
                        psum.wait_filled(act, i, ("a_proj", PAIRS - 1), "v")
                        high(i, task, "x", xT[0][:, :], psum.bank(task, "x")[:, :])
                    elif kind == "a_proj":
                        p = task[1]
                        t0, prev = earlier(task, lambda t: t[0] == "a_st" and t[1] % 2 == p % 2 and t[2] == 1)
                        psum.wait_filled(act, i, t0, 2, prev)
                        for j in range(2):
                            rows = slice(j * HEAD, (j + 1) * HEAD)
                            high(i, task, ("q", j), Qa[p % 2][0][rows, j, :], psum.bank(task, "q")[rows, :],
                                 ACT.Identity, bias=bqkv[rows, p:p + 1])
                        high(i, task, "k", Ka[p % 2][0][:, :], psum.bank(task, "k")[:, :], ACT.Identity,
                             bias=bqkv[:, PAIRS + p:PAIRS + p + 1])
                        t0, prev = earlier(task, lambda t: t[0] == "a_pv" and t[1] % 2 == p % 2 and t[2] == 1)
                        psum.wait_filled(act, i, t0, "v", prev)
                        psum.wait_filled(act, i, task, "v")
                        psum.raise_read(a.activation(
                            Va[p % 2][:, :, :, 0:HEAD],
                            psum.bank(task, "v")[:, :].rearrange("p (t j d) -> p t j d", t=TILES, j=2), ACT.Copy), task, "v")
                    elif kind in ("a_neg", "f_neg"):
                        p = task[-1]
                        st, dst = ("a_st", negT) if kind == "a_neg" else ("f_st", negfT)
                        t0, prev = earlier(task, lambda t: t[0] == st and t[-2] % 2 == p % 2 and t[-1] == 1)
                        psum.wait_filled(act, i, t0, 2 if kind == "a_neg" else 1, prev)
                        psum.wait_filled(act, i, task, "m")
                        psum.raise_read(a.activation(dst[p % 2][:, :], psum.bank(task, "m")[0:2, :].bitcast(BF16)[:, 0:SEQ],
                                                     ACT.Copy), task, "m")
                    elif kind == "a_st":
                        j = task[2]
                        t0, prev = earlier(task, lambda t: t[0] == "a_pv" and t[2] == j)
                        psum.wait_filled(act, i, t0, "v", prev)
                        for u, (at, n, _) in enumerate(CAUSAL_USES):
                            psum.wait_filled(act, i, task, u)
                            psum.raise_read(a.activation(probs[j][:, at:at + n], psum.bank(task, u)[:, 0:n], ACT.Exp,
                                                          scale=float(HEAD) ** -0.5), task, u)
                    elif kind == "f_st":
                        j = task[3]
                        t0, prev = earlier(task, lambda t: t[0] == "f_pv" and t[3] == j)
                        psum.wait_filled(act, i, t0, "v", prev)
                        for u, n in enumerate((2 * BAND, BAND + P)):
                            psum.wait_filled(act, i, task, u)
                            psum.raise_read(a.activation(lprobs[j][:, 2 * BAND * u:2 * BAND * u + n],
                                                          psum.bank(task, u)[:, 0:n], ACT.Exp), task, u)
                    elif kind == "a_ot":
                        p = task[1]
                        t0, prev = earlier(task, lambda t: t[0] == "a_out")
                        act.wait_ge(out_ready.sem, (out_ready.before if prev else out_ready.now)(i, t0, "a"))
                        high(i, task, "o", OaT[0][:, :], psum.bank(task, "o")[:, :], ACT.Identity,
                             bias=bqkv[:, 2 * PAIRS + p:2 * PAIRS + p + 1])
                    elif kind == "f_ht":
                        t0, prev = earlier(task, lambda t: t[0] == "f_up" and t[2] == LAST_UP)
                        psum.wait_filled(act, i, t0, "a", prev)
                        high(i, task, "h", hT[0][:, :], psum.bank(task, "h")[:, :])
                    elif kind == "f_qk":
                        for s, c in enumerate("qk"):
                            if s == 1:
                                psum.wait_read(act, i, task, "q")
                            else:
                                t0, prev = earlier(task, lambda t: t[0] == "f_qk" or t == ("f_up", (task[1] - 1) % DEPTH, LAST_UP))
                                psum.wait_read(act, i, t0, "k" if t0[0] == "f_qk" else "a", prev)
                            psum.wait_filled(act, i, task, c)
                            a.activation(squares, psum.bank(task, c)[:, :], ACT.Square).then_inc(squares_ready.sem, 1)
                    elif kind == "f_v":
                        t0, prev = earlier(task, lambda t: t[0] == "f_pv" and t[2:] == (LPAIRS - 1, 1))
                        psum.wait_filled(act, i, t0, "v", prev)
                        psum.wait_filled(act, i, task, "v")
                        psum.raise_read(a.activation(Vf[:, task[2], :, 0:HEAD], heads(psum.bank(task, "v")), ACT.Copy), task, "v")
                    elif kind == "f_qkt":
                        t = task[2]
                        t0, prev = earlier(task, lambda t: t[0] == "f_down")
                        psum.wait_filled(act, i, t0, "w", prev)
                        for m, dst in (("q", Qf), ("k", Kf)):
                            high(i, task, m, dst[0][:, :, t * P:(t + 1) * P],
                                 psum.bank(task, m)[:, :].rearrange("p (c n) -> p c n", n=P))
                    elif kind == "f_ot":
                        high(i, task, "o", OfT[0][:, task[2], :], psum.bank(task, "o")[:, :])
                    elif kind in ("f_wo", "f_down"):
                        if kind == "f_wo":
                            act.wait_ge(turned_ready["k"].sem, turned_ready["k"].now(i, ("f_qk", task[1], TILES - 1), "k"))
                        bias = dict(bias=b2s[:, task[1]:task[1] + 1]) if kind == "f_down" else {}
                        psum.wait_filled(act, i, task, "w")
                        psum.raise_read(a.activation(yT, psum.bank(task, "w")[:, :], ACT.Identity if bias else ACT.Copy,
                                                     **bias), task, "w")
                    elif kind == "f_ln":
                        psum.wait_read(act, i, task, "h")
                        a.activation(hT[0][:, :], ln_tmp, ACT.Copy).then_inc(hi_ready.sem, 1)
                    elif kind == "f_up":
                        _, l, j = task
                        m = HID_CHUNKS[j][1]
                        if j == 1:
                            act.wait_ge(lo_ready.sem, lo_ready.now(i, ("f_ln", l), "h"))
                        elif j > 1:
                            psum.wait_read(act, i, ("f_up", l, j - 2), "a")
                        psum.wait_filled(act, i, task, "g")
                        psum.raise_read(a.activation(gate[j % 2][0:m, :], psum.bank(task, "g")[0:m, :], ACT.Gelu,
                                                     bias=b1s[0:m, l, 1, j:j + 1]), task, "g")
                    elif kind == "f_split":
                        _, l, j = task
                        m = HID_CHUNKS[j][1]
                        psum.wait_read(act, i, ("f_up", l, j), "a")
                        a.activation(GLU[0][0:m, j, :], glu[j % 2][0:m, :], ACT.Copy).then_inc(hi_ready.sem, 1)

            before_first(act, carried["act"], lambda task: [e for sig in own["act"] for e in sig.sems(task)], steps)
            with act.Fori(0, BATCH) as i:
                steps(i, SCHEDULE)

        @block.vector
        def _(dve):
            v = nc.vector
            dve.wait_ge(params, PARAMS)
            for l in range(DEPTH):
                for kind in range(4):
                    v.tensor_tensor(rope_t[:, l, kind], rope_t[:, l, kind],
                                    scales[:, l, kind:kind + 1, :].broadcast_to([P, TILES, HEAD]), ALU.mult).then_inc(tables, 1)
            for k, (_, rows, n, parts) in enumerate(pieces):
                dve.wait_ge(staged[k % 4], 16 * (k // 4 + 1))
                dve.wait_ge(split_hi, k + 1)
                v.tensor_tensor(parts[1], scratch[0:rows, k % 4, 0:n], parts[0].bitcast(F32), ALU.subtract).then_inc(split_lo, 1)
            dve.wait_ge(tables, 4 * DEPTH)
            dve.wait_ge(split_lo, len(pieces))
            dve.wait_ge(consts, CONSTS)

            def low(i, task, mark, dst, src, hi):
                dve.wait_ge(hi_ready.sem, hi_ready.now(i, task, mark))
                psum.raise_read(v.tensor_tensor(dst, src, hi.bitcast(F32), ALU.subtract), task, mark)

            def low_biased(i, task, mark, dst, bias, hi):
                dve.wait_ge(hi_ready.sem, hi_ready.now(i, task, mark))
                psum.raise_read(v.scalar_tensor_tensor(dst, psum.bank(task, mark)[:, :], bias, hi.bitcast(F32),
                                                       ALU.add, ALU.subtract), task, mark)

            def token_norm(i, task, src):
                t0, prev = earlier(task, lambda t: t[0] in ("norm", "f_norm"))
                if prev and not isinstance(i, int):
                    dve.wait_ge(norm_ready.sem, norm_ready.before(i, t0, "n"))
                elif not prev:
                    dve.wait_ge(norm_ready.sem, norm_ready.now(i, t0, "n"))
                for t in range(TILES):
                    ins = v.bn_stats(stats[:, t, :], src[:, t, :])
                ins.then_inc(norm_ready.sem, 1)
                dve.wait_ge(norm_ready.sem, norm_ready.now(i, task, "s"))
                dve.sem_inc(carried["dve"], 1)
                for t in range(TILES):
                    ins = v.bn_aggr(mv[:, t, :], stats[:, t, :])
                ins.then_inc(norm_ready.sem, 1)
                dve.wait_ge(norm_ready.sem, norm_ready.now(i, task, "a"))
                v.tensor_scalar(var_eps[:, :], mv[:, :, 1], EPS, None, ALU.add).then_inc(norm_ready.sem, 1)
                dve.wait_ge(rstd_ready.sem, rstd_ready.now(i, task, "p"))
                for t in range(TILES):
                    ins = v.tensor_scalar(h[:, t, :], src[:, t, :], mv[:, t, 0:1], rstd[:, t:t + 1],
                                          ALU.subtract, ALU.mult)
                ins.then_inc(norm_ready.sem, 1)

            def steps(i, tasks):
                for task in tasks:
                    kind = task[0]
                    if kind == "norm":
                        dve.wait_ge(x_loaded, 16 * i + 32)
                        dve.sem_inc(carried["dve"], 1)
                        psum.wait_filled(dve, i, ("f_ln", DEPTH - 1), "h")
                        dve.sem_inc(carried["dve"], 1)
                        token_norm(i, task, x_res)
                    elif kind == "xt":
                        low(i, task, "x", xT[1][:, :], psum.bank(task, "x")[:, :], xT[0][:, :])
                    elif kind == "a_proj":
                        p = task[1]
                        dve.wait_ge(hi_ready.sem, hi_ready.now(i, task, ("q", 1)))
                        for j in range(2):
                            rows = slice(j * HEAD, (j + 1) * HEAD)
                            ins = v.scalar_tensor_tensor(Qa[p % 2][1][rows, :], psum.bank(task, "q")[rows, :],
                                                         bqkv[rows, p:p + 1], Qa[p % 2][0][rows, j, :].bitcast(F32),
                                                         ALU.add, ALU.subtract)
                        psum.raise_read(ins, task, "q")
                        low_biased(i, task, "k", Ka[p % 2][1][:, :], bqkv[:, PAIRS + p:PAIRS + p + 1], Ka[p % 2][0][:, :])
                    elif kind == "a_max":
                        p = task[1]
                        t0, prev = earlier(task, lambda t: t[0] == "a_neg" and t[1] % 2 == p % 2)
                        psum.wait_filled(dve, i, t0, "m", prev)
                        for j in range(2):
                            for u, parts in enumerate(MAX_USES):
                                psum.wait_filled(dve, i, task, (j, u))
                                for t, at in parts:
                                    ins = v.tensor_reduce(neg[p % 2][:, t, j:j + 1],
                                                          psum.bank(task, (j, u))[:, at:at + (t + 1) * P],
                                                          AX.X, ALU.max, negate=True)
                                psum.raise_read(ins, task, (j, u))
                    elif kind == "f_max":
                        p = task[2]
                        t0, prev = earlier(task, lambda t: t[0] == "f_neg" and t[2] % 2 == p % 2)
                        psum.wait_filled(dve, i, t0, "m", prev)
                        for j in range(2):
                            for u in range(2):
                                psum.wait_filled(dve, i, task, (j, u))
                                psum.raise_read(v.tensor_reduce(
                                    negf[p % 2][:, 2 * u:2 * u + 2, j],
                                    psum.bank(task, (j, u))[:, 0:2 * BAND].rearrange("p (t n) -> p t n", t=2),
                                    AX.X, ALU.max, negate=True), task, (j, u))
                    elif kind in ("a_pv", "f_pv"):
                        j = task[-1]
                        rec, dst, ot = (rec_a, Oa, "a_ot") if kind == "a_pv" else (rec_f, Of, "f_ot")
                        bank = tiles_of(psum.bank(task, "v")[:, 0:TILES * (HEAD + 1)])
                        t0, prev = earlier(task, lambda t: t[0] == kind)
                        psum.wait_read(dve, i, t0, "v", prev)
                        psum.wait_filled(dve, i, task, "v")
                        v.reciprocal(rec[:, :], bank[:, :, HEAD]).then_inc(rec_ready.sem, 1)
                        if j == 0:
                            t0, prev = earlier(task, lambda t: t[0] == ot)
                            psum.wait_filled(dve, i, t0, "o", prev)
                            if task == ("a_pv", 0, 0):
                                psum.wait_filled(dve, i, ("out",), "t", True)
                        dve.wait_ge(rec_ready.sem, rec_ready.now(i, task, "r"))
                        psum.raise_read(v.tensor_tensor(dst[:, :, j * HEAD:(j + 1) * HEAD], bank[:, :, 0:HEAD],
                                                         rec[:, :].unsqueeze(2).broadcast_to([P, TILES, HEAD]), ALU.mult),
                                         task, "v")
                    elif kind == "a_ot":
                        p = task[1]
                        low_biased(i, task, "o", OaT[1][:, :], bqkv[:, 2 * PAIRS + p:2 * PAIRS + p + 1], OaT[0][:, :])
                    elif kind == "f_ht":
                        low(i, task, "h", hT[1][:, :], psum.bank(task, "h")[:, :], hT[0][:, :])
                    elif kind == "f_qk":
                        _, l, t = task
                        hh = HEAD // 2
                        for s, c in enumerate("qk"):
                            dve.wait_ge(squares_ready.sem, squares_ready.now(i, task, c))
                            src = heads(psum.bank(task, c))

                            def table(term, a, b):
                                return rope_t[:, l, 2 * s + term, t, a:b].unsqueeze(1).broadcast_to([P, LHEADS, b - a])

                            if s == 1:
                                dve.wait_ge(turned_ready["q"].sem, turned_ready["q"].now(i, task, "q"))
                            elif t > 0:
                                dve.wait_ge(turned_ready["k"].sem, turned_ready["k"].now(i, ("f_qk", l, t - 1), "k"))
                            elif l > 0:
                                dve.wait_ge(lo_ready.sem, lo_ready.now(i, ("f_split", l - 1, LAST_UP), "g"))
                            else:
                                dve.wait_ge(stored, 16 * i + 16)
                            if s == 0 and t == 0:
                                t0, prev = earlier(task, lambda t: t[0] == "f_split" and t[2] == LAST_UP)
                                dve.wait_ge(hi_ready.sem, (hi_ready.before if prev else hi_ready.now)(i, t0, "g"))
                            v.tensor_tensor(heads(turn_a), src, table(0, 0, HEAD), ALU.mult)
                            tb = heads(turn_b)
                            v.tensor_tensor(tb[:, :, 0:hh], src[:, :, hh:HEAD], table(1, 0, hh), ALU.mult)
                            v.tensor_tensor(tb[:, :, hh:HEAD], src[:, :, 0:hh], table(1, hh, HEAD), ALU.mult).then_inc(turn_ready.sem, 1)
                            psum.raise_read(v.tensor_reduce(ss[:, :], heads(squares), AX.X, ALU.add), task, c)
                            psum.wait_read(dve, i, task, c)
                            v.tensor_scalar(ssc[s][:, :], ss[:, :], 1e-24, None, ALU.max).then_inc(clip_ready.sem, 1)
                            if c == "q":
                                if task[1:] == (0, 0):
                                    dve.wait_ge(sum_ready.sem, sum_ready.before(i, ("out",), "o"))
                                t0, prev = earlier(task, lambda t: t[0] == "f_qk")
                                dve.wait_ge(qk_ready.sem, (qk_ready.before if prev else qk_ready.now)(i, t0, "k"))
                                dve.wait_ge(turn_ready.sem, turn_ready.now(i, task, c))
                                v.tensor_tensor(turned, turn_a, turn_b, ALU.add).then_inc(turned_ready[c].sem, 1)
                    elif kind == "f_qkt":
                        t = task[2]
                        for m, dst in (("q", Qf), ("k", Kf)):
                            low(i, task, m, dst[1][:, :, t * P:(t + 1) * P],
                                psum.bank(task, m)[:, :].rearrange("p (c n) -> p c n", n=P), dst[0][:, :, t * P:(t + 1) * P])
                    elif kind == "f_ot":
                        low(i, task, "o", OfT[1][:, task[2], :], psum.bank(task, "o")[:, :], OfT[0][:, task[2], :])
                    elif kind in ("f_wot", "f_downt"):
                        if kind == "f_wot":
                            dve.wait_ge(shifted, shifts_done(i, ("f_ht", task[1])))
                        psum.wait_filled(dve, i, task, "t")
                        psum.raise_read(v.tensor_tensor(xl[:, :, :], tiles_of(psum.bank(task, "t")), xl[:, :, :], ALU.add), task, "t")
                    elif kind == "f_norm":
                        dve.wait_ge(shifted, shifts_done(i, task))
                        dve.sem_inc(carried["dve"], 1)
                        token_norm(i, task, h)
                    elif kind == "f_ln":
                        l = task[1]
                        psum.wait_filled(dve, i, task, "h")
                        psum.raise_read(v.tensor_scalar(ln_tmp, psum.bank(task, "h")[:, :], lng[:, l:l + 1],
                                                        lnb[:, l:l + 1], ALU.mult, ALU.add), task, "h")
                        dve.wait_ge(hi_ready.sem, hi_ready.now(i, task, "h"))
                        v.tensor_tensor(hT[1][:, :], ln_tmp, hT[0][:, :].bitcast(F32), ALU.subtract).then_inc(lo_ready.sem, 1)
                    elif kind == "f_up":
                        _, l, j = task
                        m = HID_CHUNKS[j][1]
                        if j > 1:
                            dve.wait_ge(hi_ready.sem, hi_ready.now(i, ("f_split", l, j - 2), "g"))
                            dve.wait_ge(lo_ready.sem, lo_ready.now(i, ("f_split", l, j - 2), "g"))
                        psum.wait_read(dve, i, task, "g")
                        psum.wait_filled(dve, i, task, "a")
                        psum.raise_read(v.scalar_tensor_tensor(glu[j % 2][0:m, :], psum.bank(task, "a")[0:m, :],
                                                               b1s[0:m, l, 0, j:j + 1], gate[j % 2][0:m, :],
                                                               ALU.add, ALU.mult), task, "a")
                    elif kind == "f_split":
                        _, l, j = task
                        m = HID_CHUNKS[j][1]
                        dve.wait_ge(hi_ready.sem, hi_ready.now(i, task, "g"))
                        v.tensor_tensor(GLU[1][0:m, j, :], glu[j % 2][0:m, :], GLU[0][0:m, j, :].bitcast(F32),
                                        ALU.subtract).then_inc(lo_ready.sem, 1)
                    elif kind == "a_end":
                        dve.wait_ge(out_ready.sem, out_ready.now(i, ("a_out", PAIRS - 1), "a"))
                        v.tensor_scalar(aT, out_acc[:, :], bout[:, 0:1], None, ALU.add).then_inc(aT_ready.sem, 1)
                    elif kind == "out":
                        psum.wait_filled(dve, i, task, "t")
                        psum.raise_read(v.tensor_tensor(out_a, tiles_of(psum.bank(task, "t")), xl[:, :, :], ALU.add), task, "t")

            before_first(dve, carried["dve"], lambda task: [e for sig in own["dve"] for e in sig.sems(task)] + psum.sems(task, psum.read),
                         steps)
            with dve.Fori(0, BATCH) as i:
                steps(i, SCHEDULE)

        @block.tensor
        def _(pe):
            mm = nc.tensor.matmul
            pe.wait_ge(consts, CONSTS)
            pe.wait_ge(split_lo, len(pieces))

            def product(dst, left, right, first=True, last=True):
                mm(dst, left[0], right[0], start=first, stop=False)
                mm(dst, left[1], right[0], start=False, stop=False)
                return mm(dst, left[0], right[1], start=False, stop=last)

            def parts(pair, *index):
                return [t[index] for t in pair]

            def transposes(i, task, mark, src, after=()):
                bank = psum.claim(pe, i, task, mark, after)
                for t in range(TILES):
                    ins = nc.tensor.transpose(bank[:, t * P:(t + 1) * P], src(t), ident[:, :])
                psum.raise_filled(ins, task, mark)

            def wait_parts(i, task, mark):
                pe.wait_ge(hi_ready.sem, hi_ready.now(i, task, mark))
                if (task, mark) in lo_ready.at:
                    pe.wait_ge(lo_ready.sem, lo_ready.now(i, task, mark))
                    return []
                return [(task, mark)]

            ALLP = slice(0, P)

            def tile(t):
                return slice(t * P, (t + 1) * P)

            def steps(i, tasks):
                for task in tasks:
                    kind = task[0]
                    if kind == "xt":
                        pe.wait_ge(norm_ready.sem, norm_ready.now(i, ("norm",), "n"))
                        transposes(i, task, "x", lambda t: h[:, t, :])
                    elif kind == "a_proj":
                        p = task[1]
                        if p == 0:
                            pe.wait_ge(hi_ready.sem, hi_ready.before(i, ("xt",), "x"))
                            psum.wait_read(pe, i, ("xt",), "x", True)
                            pe.sem_inc(carried["pe"], 1)
                        for c, m in enumerate("qk"):
                            bank = psum.claim(pe, i, task, m)
                            cols = slice(c * HEADS * HEAD + p * P, c * HEADS * HEAD + (p + 1) * P)
                            psum.raise_filled(product(bank[:, :], parts(Wqkv, ALLP, cols), parts(xT, ALLP)), task, m)
                        bank = psum.claim(pe, i, task, "v")
                        cols = slice(2 * HEADS * HEAD + p * P, 2 * HEADS * HEAD + (p + 1) * P)
                        for t in range(TILES):
                            ins = product(bank[:, tile(t)], parts(xT, ALLP, tile(t)), parts(Wqkv, ALLP, cols))
                        psum.raise_filled(ins, task, "v")
                    elif kind == "a_max":
                        p = task[1]
                        pe.wait_ge(hi_ready.sem, hi_ready.now(i, ("a_proj", p), "k"))
                        Q, K = Qa[p % 2][0], Ka[p % 2][0]
                        for j in range(2):
                            for u, uses in enumerate(MAX_USES):
                                bank = psum.claim(pe, i, task, (j, u))
                                for t, at in uses:
                                    n = (t + 1) * P
                                    mm(bank[:, at:at + n], Q[:, j, tile(t)], K[:, 0:n], start=True, stop=False)
                                    ins = mm(bank[:, at + n - P:at + n], mask_row[:, :], future_q[:, :], start=False, stop=True)
                                psum.raise_filled(ins, task, (j, u))
                    elif kind == "f_max":
                        _, l, p = task
                        if p == 0:
                            pe.wait_ge(hi_ready.sem, hi_ready.now(i, ("f_qkt", l, TILES - 1), "k"))
                        for j in range(2):
                            rows = slice(j * HEAD, (j + 1) * HEAD)
                            for u in range(2):
                                bank = psum.claim(pe, i, task, (j, u))
                                mm(bank[:, 0:2 * BAND], mask_row[:, :], band[:, u:u + 2, :].rearrange("p a n -> p (a n)"),
                                   start=True, stop=False)
                                for k in range(2):
                                    t = 2 * u + k
                                    k0 = t * P - WINDOW if t else 0
                                    at = k * BAND + (0 if t else WINDOW)
                                    ins = mm(bank[:, at:(k + 1) * BAND], Qf[0][rows, p, tile(t)],
                                             Kf[0][rows, p, k0:(t + 1) * P], start=False, stop=(k == 1))
                                psum.raise_filled(ins, task, (j, u))
                    elif kind in ("a_neg", "f_neg"):
                        src, other, u = (neg, "a_max", 2) if kind == "a_neg" else (negf, "f_max", 1)
                        bank = psum.claim(pe, i, task, "m", [((other, *task[1:]), (1, k)) for k in range(u + 1)])[0:2, :].bitcast(BF16)
                        for t in range(TILES):
                            ins = nc.tensor.transpose(bank[:, tile(t)], src[task[-1] % 2][:, t, :], identb[:, :])
                        psum.raise_filled(ins, task, "m")
                    elif kind == "a_st":
                        p, j = task[1], task[2]
                        rows = slice(j * HEAD, (j + 1) * HEAD)
                        after = [(("a_proj", p), "q"), (("a_proj", p), "k"), (("a_neg", p), "m")] if j == 0 else []
                        for u, (_, _, uses) in enumerate(CAUSAL_USES):
                            bank = psum.claim(pe, i, task, u, after if u == 0 else [])
                            for k, at in uses:
                                n = SEQ - k * P
                                queries = slice(k * P, SEQ)
                                (Qhi, Qlo), (Khi, Klo) = Qa[p % 2], Ka[p % 2]
                                dst = bank[:, at:at + n]
                                mm(dst, Khi[:, tile(k)], Qhi[:, j, queries], start=True, stop=False)
                                mm(dst, Klo[:, tile(k)], Qhi[:, j, queries], start=False, stop=False)
                                mm(dst, Khi[rows, tile(k)], Qlo[rows, queries], start=False, stop=False)
                                mm(bank[:, at:at + n], pick[:, j, :], negT[p % 2][:, queries], start=False, stop=False)
                                ins = mm(bank[:, at:at + P], mask_row[:, :], future_k[:, :], start=False, stop=True)
                            psum.raise_filled(ins, task, u)
                    elif kind == "f_st":
                        _, l, p, j = task
                        rows = slice(j * HEAD, (j + 1) * HEAD)
                        after = [(("f_neg", l, p), "m")] if j == 0 else []
                        if j == 0 and p == 0:
                            after += [(("f_qkt", l, t), m) for t in range(TILES) for m in "qk"]
                        for u in range(2):
                            bank = psum.claim(pe, i, task, u, after if u == 0 else [])
                            total = 2 * BAND if u == 0 else BAND + P
                            mm(bank[:, 0:total], mask_row[:, :], band[:, 1:3, :].rearrange("p a n -> p (a n)")[:, 0:total],
                               start=True, stop=False)
                            for k in range(2):
                                t = 2 * u + k
                                n = min(BAND, SEQ - t * P)
                                dst = bank[:, k * BAND:k * BAND + n]
                                queries = slice(t * P, t * P + n)
                                product(dst, parts(Kf, rows, p, tile(t)), parts(Qf, rows, p, queries), first=False, last=False)
                                ins = mm(dst, pick[:, j, :], negfT[p % 2][:, queries], start=False, stop=(k == 1))
                            psum.raise_filled(ins, task, u)
                    elif kind == "a_pv":
                        p, j = task[1], task[2]
                        bank = psum.claim(pe, i, task, "v", [(("a_proj", p), "v")] + [(("a_st", p, j), u) for u in range(3)])
                        for t in range(TILES):
                            for k in range(t + 1):
                                at = CAUSAL_AT[k] + (t - k) * P
                                ins = mm(bank[:, t * (HEAD + 1):(t + 1) * (HEAD + 1)], probs[j][:, at:at + P],
                                         Va[p % 2][:, k, j, :], start=(k == 0), stop=(k == t))
                        psum.raise_filled(ins, task, "v")
                    elif kind == "f_pv":
                        _, l, p, j = task
                        after = [(("f_st", l, p, j), u) for u in range(2)]
                        if p == 0 and j == 0:
                            after += [(("f_v", l, t), "v") for t in range(TILES)]
                        bank = psum.claim(pe, i, task, "v", after)
                        for t in range(TILES):
                            to = bank[:, t * (HEAD + 1):(t + 1) * (HEAD + 1)]
                            ins = mm(to, lprobs[j][:, t * BAND:t * BAND + P], Vf[:, t, 2 * p + j, :], start=True, stop=True)
                            if t > 0:
                                ins = mm(to[0:WINDOW], lprobs[j][:, t * BAND - WINDOW:t * BAND], Vf[:, t - 1, 2 * p + j, :],
                                         start=False, stop=True, skip_group_check=True)
                        psum.raise_filled(ins, task, "v")
                    elif kind == "a_ot":
                        transposes(i, task, "o", lambda t: Oa[:, t, :], [(("a_pv", task[1], 1), "v")])
                    elif kind == "f_ot":
                        transposes(i, task, "o", lambda t: Of[:, t, :], [(("f_pv", task[1], task[2], 1), "v")])
                    elif kind == "a_out":
                        p = task[1]
                        psum.wait_all_read(pe, i, wait_parts(i, ("a_ot", p), "o"))
                        if p == 0:
                            pe.wait_ge(aT_ready.sem, aT_ready.before(i, ("a_end",), "a"))
                        product(out_acc[:, :], parts(Wout, ALLP, p), parts(OaT, ALLP), first=(p == 0),
                                last=(p == PAIRS - 1)).then_inc(out_ready.sem, 1)
                    elif kind == "f_ht":
                        pe.wait_ge(shifted, shifts_done(i, task))
                        pe.wait_ge(zeroed, i * (16 * DEPTH) + 16 * (task[1] + 1))
                        transposes(i, task, "h", lambda t: h[:, t, :])
                    elif kind == "f_qk":
                        _, l, t = task
                        after = wait_parts(i, ("f_ht", l), "h") if t == 0 else []
                        for c, m in enumerate("qk"):
                            bank = psum.claim(pe, i, task, m, after if m == "q" else [])
                            psum.raise_filled(product(bank[:, :], parts(hT, ALLP, tile(t)),
                                                      parts(Lqkv[l], ALLP, slice(c * INNER, (c + 1) * INNER))), task, m)
                    elif kind == "f_v":
                        _, l, t = task
                        bank = psum.claim(pe, i, task, "v")
                        psum.raise_filled(product(bank[:, :], parts(hT, ALLP, tile(t)),
                                                  parts(Lqkv[l], ALLP, slice(2 * INNER, 3 * INNER))), task, "v")
                    elif kind == "f_qkt":
                        _, l, t = task
                        for s, m in enumerate("qk"):
                            pe.wait_ge(qk_ready.sem, qk_ready.now(i, ("f_qk", l, t), m))
                            transposes(i, task, m, lambda c: qkn[s][:, tile(c)])
                    elif kind == "f_wo":
                        l = task[1]
                        bank = psum.claim(pe, i, task, "w", wait_parts(i, ("f_ot", l, LPAIRS - 1), "o"))
                        for c in range(LPAIRS):
                            ins = product(bank[:, :], parts(Lwo[l], ALLP, c), parts(OfT, ALLP, c),
                                          first=(c == 0), last=(c == LPAIRS - 1))
                        psum.raise_filled(ins, task, "w")
                    elif kind in ("f_wot", "f_downt"):
                        transposes(i, task, "t", lambda t: yT[:, tile(t)], [((kind[:-1], task[1]), "w")])
                    elif kind == "f_ln":
                        pe.wait_ge(norm_ready.sem, norm_ready.now(i, ("f_norm", task[1]), "n"))
                        transposes(i, task, "h", lambda t: h[:, t, :])
                    elif kind == "f_up":
                        _, l, j = task
                        c, m = HID_CHUNKS[j]
                        if j == 0:
                            wait_parts(i, ("f_ln", l), "h")
                        for half, mark in ((1, "g"), (0, "a")):
                            bank = psum.claim(pe, i, task, mark)
                            at = half * HID + c
                            psum.raise_filled(product(bank[0:m, :], parts(Lw1[l], ALLP, slice(at, at + m)), parts(hT, ALLP)),
                                              task, mark)
                    elif kind == "f_down":
                        l = task[1]
                        wait_parts(i, ("f_split", l, LAST_UP), "g")
                        bank = psum.claim(pe, i, task, "w")
                        for j, (c, m) in enumerate(HID_CHUNKS):
                            ins = product(bank[:, :], parts(Lw2[l], slice(0, m), j), parts(GLU, slice(0, m), j),
                                          first=(j == 0), last=(j == LAST_UP))
                        psum.raise_filled(ins, task, "w")
                    elif kind == "out":
                        pe.wait_ge(aT_ready.sem, aT_ready.now(i, ("a_end",), "a"))
                        transposes(i, task, "t", lambda t: aT[:, tile(t)])

            before_first(pe, carried["pe"], lambda task: [e for sig in own["pe"] for e in sig.sems(task)] + psum.sems(task, psum.filled),
                         steps)
            with pe.Fori(0, BATCH) as i:
                steps(i, SCHEDULE)


PARAMS = 16 * (5 + DEPTH * (2 * len(HID_CHUNKS) + 6 + 4))
CONSTS = 24

_INS = ["L0_attn_x", "L0_attn_W_qkv", "L0_attn_b_qkv", "L0_attn_W_out", "L0_attn_b_out", "L0_ffn_wqkv",
        "L0_ffn_q_scale", "L0_ffn_k_scale", "L0_ffn_wo", "L0_ffn_ln_g", "L0_ffn_ln_b", "L0_ffn_w1", "L0_ffn_b1",
        "L0_ffn_w2", "L0_ffn_b2"]


def kernel(**inputs):
    import numpy as _np
    import concourse.bacc as _bacc
    from concourse import mybir as _mybir
    from concourse.bass_utils import run_bass_kernel_spmd as _run

    nc = _bacc.Bacc("TRN2", target_bir_lowering=False, num_devices=1)
    arrays, args = {}, []
    for name in _INS:
        a = _np.ascontiguousarray(inputs[name])
        arrays[f"in_{name}"] = a
        args.append(nc.dram_tensor(f"in_{name}", a.shape, _mybir.dt.from_np(a.dtype), kind="ExternalInput").ap())
    rope = rope_tables()
    arrays["in_rope"] = rope
    args.append(nc.dram_tensor("in_rope", rope.shape, _mybir.dt.float32, kind="ExternalInput").ap())
    out = nc.dram_tensor("out_0", (BATCH, SEQ, DIM), _mybir.dt.float32, kind="ExternalOutput").ap()
    prenorm_attention_and_local_transformer(nc, *args, out)
    r = _run(nc, [arrays], core_ids=[0])
    return r.results[0]["out_0"]
```
